# Optimizing a Trainium2 kernel written in Bass

```python
import numpy as np
import jax
import jax.numpy as jnp

def _softmax(x, axis=-1):
    return jax.nn.softmax(x, axis=axis)

def _gelu(x):
    return jax.nn.gelu(x, approximate=True)

def _silu(x):
    return jax.nn.silu(x)

def _sigmoid(x):
    return jax.nn.sigmoid(x)

def _layernorm(x, axis=-1, eps=1e-05):
    m = jnp.mean(x, axis=axis, keepdims=True)
    v = jnp.var(x, axis=axis, keepdims=True)
    return (x - m) / jnp.sqrt(v + eps)

def _scatter_add(tgt, idx, src, axis=0):
    return tgt.at[idx].add(src)

def _segment_sum(src, seg, n):
    return jax.ops.segment_sum(src, seg, n)
kernel_name = 'mk_perceiver_d1_seqx_r8_1392eb'

def setup_inputs(seed: int=0):
    np.random.seed(seed)
    _w = jnp.asarray

    def _rec_inputs():
        import jax
        import jax.numpy as jnp
        _rk = jax.random.key(seed)
        x = 7.22e-05 + 1 * jax.random.normal(jax.random.fold_in(_rk, 1), (4, 128, 128), jnp.float32)
        _lenS = 128 - jax.random.randint(jax.random.fold_in(_rk, 7), (4,), 0, max(1, 128 // 4) + 1, jnp.int32)
        _lenS2 = 2048 - jax.random.randint(jax.random.fold_in(_rk, 8), (4,), 0, max(1, 2048 // 4) + 1, jnp.int32)
        _ctx_1024P = jax.random.normal(jax.random.fold_in(_rk, 11), (4, 16, 128), jnp.float32)
        _ctx_1024c = jax.random.dirichlet(jax.random.fold_in(_rk, 511), 0.3 * jnp.ones((16,), jnp.float32), (4, 2048))
        _ctx_1024t = jnp.einsum('bsk,bkd->bsd', _ctx_1024c, _ctx_1024P)
        _ctx_1024t = _ctx_1024t * jax.lax.rsqrt(jnp.mean(jnp.square(_ctx_1024t)) + 1e-12) * 0.953939
        ctx_1024 = 4.13588e-05 + 0.999923 * (_ctx_1024t + 0.3 * jax.random.normal(jax.random.fold_in(_rk, 611), (4, 2048, 128), jnp.float32))
        return (x, ctx_1024)
    x, ctx_1024 = _rec_inputs()

    def _L0_xattn_setup():
        import jax, jax.numpy as jnp
        import numpy as np
        D_MODEL = 128
        DK = 64
        N_HEADS = D_MODEL // DK
        MASK = True
        key = jax.random.key(seed)
        ks = jax.random.split(key, 8)
        B, S = (4, 256)
        scale = 1.0 / np.sqrt(D_MODEL)
        return {'query_data': jax.random.normal(ks[0], (B, S, D_MODEL), dtype=jnp.float32), 'key_data': jax.random.normal(ks[1], (B, S, D_MODEL), dtype=jnp.float32), 'value_data': jax.random.normal(ks[2], (B, S, D_MODEL), dtype=jnp.float32), 'Wq': jax.random.normal(ks[3], (D_MODEL, D_MODEL), dtype=jnp.float32) * scale, 'Wk': jax.random.normal(ks[4], (D_MODEL, D_MODEL), dtype=jnp.float32) * scale, 'Wv': jax.random.normal(ks[5], (D_MODEL, D_MODEL), dtype=jnp.float32) * scale, 'Wp': jax.random.normal(ks[6], (D_MODEL, D_MODEL), dtype=jnp.float32) * scale, 'bp': jnp.zeros((D_MODEL,), dtype=jnp.float32)}
    _L0_xattn_all = _L0_xattn_setup()
    _L0_xattn_in = {k: v for k, v in _L0_xattn_all.items() if k in ('Wq', 'Wk', 'Wv', 'Wp', 'bp')}
    del _L0_xattn_all

    def _L0_attn_setup():
        import jax, jax.numpy as jnp
        import numpy as np
        H = 16

        def _toroidal_bias(S, dtype):
            eye = jnp.eye(S, dtype=dtype)
            return eye + jnp.roll(eye, 1, axis=1) + jnp.roll(eye, -1, axis=1)
        key = jax.random.key(seed)
        ks = jax.random.split(key, 7)
        E = 128
        S, B = (256, 2)
        sc = 0.02
        return {'x': jax.random.normal(ks[0], (S, B, E), dtype=jnp.float32), 'w_tor': jax.random.normal(ks[1], (E, E), dtype=jnp.float32) * sc, 'b_tor': jax.random.normal(ks[2], (E,), dtype=jnp.float32) * sc, 'in_proj_w': jax.random.normal(ks[3], (3 * E, E), dtype=jnp.float32) * sc, 'in_proj_b': jax.random.normal(ks[4], (3 * E,), dtype=jnp.float32) * sc, 'out_w': jax.random.normal(ks[5], (E, E), dtype=jnp.float32) * sc, 'out_b': jax.random.normal(ks[6], (E,), dtype=jnp.float32) * sc}
    _L0_attn_all = _L0_attn_setup()
    _L0_attn_in = {k: v for k, v in _L0_attn_all.items() if k in ('w_tor', 'b_tor', 'in_proj_w', 'in_proj_b', 'out_w', 'out_b')}
    del _L0_attn_all

    def _L0_ffn_setup():
        import jax, jax.numpy as jnp
        import numpy as np
        SL, BS, HS, FF, E, TOPK = (256, 2, 128, 512, 8, 2)
        key = jax.random.key(seed)
        ks = jax.random.split(key, 6)
        T = SL * BS
        x = jax.random.normal(ks[0], (SL, BS, HS), jnp.float32)
        scores = jax.random.uniform(ks[1], (T, E), jnp.float32)
        expert_weights = jax.random.uniform(ks[2], (T, TOPK), jnp.float32)
        expert_indices = jax.random.randint(ks[3], (T, TOPK), 0, E, jnp.int32)
        w1 = jax.random.normal(ks[4], (E, HS, FF), jnp.float32) * (1.0 / np.sqrt(HS))
        w2 = jax.random.normal(ks[5], (E, FF, HS), jnp.float32) * (1.0 / np.sqrt(FF))
        bias = jnp.zeros((HS,), jnp.float32)
        return dict(x=x, scores=scores, expert_weights=expert_weights, expert_indices=expert_indices, w1=w1, w2=w2, bias=bias)
    _L0_ffn_all = _L0_ffn_setup()
    _L0_ffn_in = {k: v for k, v in _L0_ffn_all.items() if k in ('scores', 'expert_weights', 'expert_indices', 'w1', 'w2', 'bias')}
    del _L0_ffn_all
    return {'x': x, 'ctx_1024': ctx_1024, 'L0_xattn_Wq': _L0_xattn_in['Wq'], 'L0_xattn_Wk': _L0_xattn_in['Wk'], 'L0_xattn_Wv': _L0_xattn_in['Wv'], 'L0_xattn_Wp': _L0_xattn_in['Wp'], 'L0_xattn_bp': _L0_xattn_in['bp'], 'L0_attn_w_tor': _L0_attn_in['w_tor'], 'L0_attn_b_tor': _L0_attn_in['b_tor'], 'L0_attn_in_proj_w': _L0_attn_in['in_proj_w'], 'L0_attn_in_proj_b': _L0_attn_in['in_proj_b'], 'L0_attn_out_w': _L0_attn_in['out_w'], 'L0_attn_out_b': _L0_attn_in['out_b'], 'L0_ffn_scores': _L0_ffn_in['scores'], 'L0_ffn_expert_weights': _L0_ffn_in['expert_weights'], 'L0_ffn_expert_indices': _L0_ffn_in['expert_indices'], 'L0_ffn_w1': _L0_ffn_in['w1'], 'L0_ffn_w2': _L0_ffn_in['w2'], 'L0_ffn_bias': _L0_ffn_in['bias']}

def reference(x, ctx_1024, L0_xattn_Wq, L0_xattn_Wk, L0_xattn_Wv, L0_xattn_Wp, L0_xattn_bp, L0_attn_w_tor, L0_attn_b_tor, L0_attn_in_proj_w, L0_attn_in_proj_b, L0_attn_out_w, L0_attn_out_b, L0_ffn_scores, L0_ffn_expert_weights, L0_ffn_expert_indices, L0_ffn_w1, L0_ffn_w2, L0_ffn_bias):
    import jax
    import jax.numpy as jnp

    def _L0_xattn_ref(query_data, key_data, value_data, Wq, Wk, Wv, Wp, bp):
        import jax, jax.numpy as jnp
        import numpy as np
        D_MODEL = 128
        DK = 64
        N_HEADS = D_MODEL // DK
        MASK = True
        B, S, _ = query_data.shape

        def split_heads(x, W):
            return (x @ W.T).reshape(B, -1, N_HEADS, DK).transpose(0, 2, 1, 3)
        q = split_heads(query_data, Wq)
        k = split_heads(key_data, Wk)
        v = split_heads(value_data, Wv)
        scores = jnp.einsum('bhqd,bhkd->bhqk', q, k) / np.sqrt(DK).astype(np.float32)
        if MASK:
            Sq, Sk = (scores.shape[-2], scores.shape[-1])
            causal = jnp.triu(jnp.ones((Sq, Sk), dtype=scores.dtype), k=1) * jnp.float32(-10000000000000.0)
            scores = scores + causal
        attn = jax.nn.softmax(scores, axis=-1)
        out = jnp.einsum('bhqk,bhkd->bhqd', attn, v)
        out = out.transpose(0, 2, 1, 3).reshape(B, S, D_MODEL)
        return out @ Wp.T + bp

    def _L0_attn_ref(x, w_tor, b_tor, in_proj_w, in_proj_b, out_w, out_b):
        import jax, jax.numpy as jnp
        import numpy as np
        H = 16

        def _toroidal_bias(S, dtype):
            eye = jnp.eye(S, dtype=dtype)
            return eye + jnp.roll(eye, 1, axis=1) + jnp.roll(eye, -1, axis=1)
        S, B, E = x.shape
        hd = E // H
        scale = 1.0 / jnp.sqrt(jnp.asarray(hd, dtype=x.dtype))
        xt = x @ w_tor.T + b_tor
        qkv = xt @ in_proj_w.T + in_proj_b
        q, k, v = jnp.split(qkv, 3, axis=-1)

        def to_heads(t):
            return t.reshape(S, B, H, hd).transpose(1, 2, 0, 3)
        q, k, v = (to_heads(q), to_heads(k), to_heads(v))
        bias = _toroidal_bias(S, x.dtype)
        scores = jnp.einsum('bhqd,bhkd->bhqk', q * scale, k) + bias
        attn = jax.nn.softmax(scores, axis=-1)
        o = jnp.einsum('bhqk,bhkd->bhqd', attn, v)
        o = o.transpose(2, 0, 1, 3).reshape(S, B, E)
        return o @ out_w.T + out_b

    def _L0_ffn_ref(x, scores, expert_weights, expert_indices, w1, w2, bias):
        import jax, jax.numpy as jnp
        import numpy as np
        SL, BS, HS, FF, E, TOPK = (256, 2, 128, 512, 8, 2)
        sl, bs, hs = x.shape
        n_exp = w1.shape[0]
        top_k = expert_indices.shape[-1]
        xf = x.reshape(-1, hs)
        flat_idx = expert_indices.reshape(-1)
        flat_w = expert_weights.reshape(-1)
        order = jnp.argsort(flat_idx)
        tok = order // top_k
        tokens_per_expert = jnp.bincount(flat_idx, length=n_exp).astype(jnp.int32)
        xs = xf[tok]
        h = jax.nn.gelu(jax.lax.ragged_dot(xs, w1, tokens_per_expert), approximate=False)
        ys = jax.lax.ragged_dot(h, w2, tokens_per_expert)
        ys = ys * flat_w[order][:, None]
        out = jnp.zeros_like(xf).at[tok].add(ys)
        return out.reshape(sl, bs, hs) + bias
    x = x + _L0_xattn_ref(_layernorm(x, axis=-1), ctx_1024, ctx_1024, L0_xattn_Wq, L0_xattn_Wk, L0_xattn_Wv, L0_xattn_Wp, L0_xattn_bp)
    x = x + _L0_attn_ref(_layernorm(x, axis=-1), L0_attn_w_tor, L0_attn_b_tor, L0_attn_in_proj_w, L0_attn_in_proj_b, L0_attn_out_w, L0_attn_out_b)
    x = x + _L0_ffn_ref(_layernorm(x, axis=-1), L0_ffn_scores, L0_ffn_expert_weights, L0_ffn_expert_indices, L0_ffn_w1, L0_ffn_w2, L0_ffn_bias)
    return x

_drawn_inputs = setup_inputs


def setup_inputs(seed=0):
    import zlib

    import numpy as np

    out = dict(_drawn_inputs(seed))
    spreads = {'L0_xattn_bp': (0.0, 0.1), 'L0_ffn_bias': (0.0, 0.497)}
    factors = {'L0_attn_w_tor': 8.0,
     'L0_attn_b_tor': 8.0,
     'L0_attn_in_proj_w': 8.0,
     'L0_attn_in_proj_b': 8.0,
     'L0_attn_out_w': 8.0,
     'L0_attn_out_b': 16.58}
    for name, (base, spread) in spreads.items():
        noise = np.random.default_rng([zlib.crc32(name.encode()), seed]).standard_normal(out[name].shape)
        drawn = base * np.exp(spread * noise) if base else spread * noise
        out[name] = jnp.asarray(drawn.astype(out[name].dtype))
    for name, factor in factors.items():
        out[name] = (out[name] * factor).astype(out[name].dtype)
    return out
```

```python
from contextlib import ExitStack

import concourse.bass as bass
from concourse import mybir

ALU = mybir.AluOpType
ACT = mybir.ActivationFunctionType
AX = mybir.AxisListType
F32 = mybir.dt.float32
I32 = mybir.dt.int32


def perceiver_layer(nc, x, ctxT, w_cross, w_self, cols, rows, exp_idx, exp_wt, w1, w2, out):
    S, B, D = x.shape
    XH, DK = 2, D // 2
    H, HD = 16, D // 16
    E, FF = w1.shape[1:]
    FC = FF // 128
    TOPK = 2
    BIG = 1.0e13
    EPS = 1e-5
    FOLD_BANK = [0, 3]
    KQ_BANK = [1, 2]
    XNT_BANK = 5
    WQKV_BANK = 4
    VP_BANK = [0, 3]
    SCORE_BANK = [6, 7, 5, 1]
    PROBT_BANK = [2, 6, 7, 5]
    XO_BANK = [0, 3, 1, 2]
    XNT1_BANK = [4, 6, 7, 5]
    QV_BANK = [0, 3, 1, 6]
    K_BANK = [4, 7]
    OB_BANK = 2
    SC_BANK = 5
    OT_BANK = [0, 3, 1, 4]
    SO_BANK = [6, 7, 2, 5]
    XNT2_BANK = [0, 3, 1, 4]
    H_BANK = [6, 7, 2, 5]
    Y_BANK = [0, 3, 1, 4]

    with ExitStack() as ctx:
        def sb(name, shape, dt=F32):
            return ctx.enter_context(nc.sbuf_tensor(name, shape, dt))

        def sem(name):
            return ctx.enter_context(nc.semaphore(name))

        bank = [ctx.enter_context(nc.psum_tensor(f"bank{i}", [128, 512], F32)) for i in range(8)]

        x_sb = sb("x_sb", [128, S, D])
        ctx_sb = sb("ctx_sb", [128, S, B])
        wc_sb = sb("wc_sb", [128, 4, D])
        ws_sb = sb("ws_sb", [128, 5, D])
        col_sb = sb("col_sb", [128, 4])
        row_sb = sb("row_sb", [128, 3, D])
        idx_sb = sb("idx_sb", [128, S, TOPK], I32)
        wt_sb = sb("wt_sb", [128, S, TOPK])
        w1_sb = sb("w1_sb", [128, E, FF])
        w2_sb = sb("w2_sb", [128, E, FC, D])

        ident = sb("ident", [128, 128])
        mask = sb("mask", [128, XH, B])
        tor = sb("tor", [128, S, S])
        head_sel = sb("head_sel", [128, H])
        half = sb("half", [128, S])

        fold_sb = sb("fold_sb", [128, 2, XH, D])
        kq_sb = sb("kq_sb", [128, S, XH, B])
        vp_sb = sb("vp_sb", [128, S, XH, D])
        wqkv_sb = sb("wqkv_sb", [128, 3, D])
        bqkv = sb("bqkv", [128, 3])
        bq_scaled = sb("bq_scaled", [128, 1])
        bv_wide = sb("bv_wide", [128, 128])
        out_bias = sb("out_bias", [128, D])
        gate = sb("gate", [128, S, E])
        iota_e = sb("iota_e", [128, E])
        idx_f = sb("idx_f", [128, S, TOPK])
        pick = sb("pick", [128, TOPK, S, E])
        pick_w = sb("pick_w", [128, TOPK, S, E])

        stats = [sb(f"stats{i}", [128, S, 6]) for i in range(3)]
        mv = [sb(f"mv{i}", [128, S, 2]) for i in range(3)]
        var_eps = [sb(f"var_eps{i}", [128, S]) for i in range(3)]
        rstd = [sb(f"rstd{i}", [128, S]) for i in range(3)]
        xn = [sb(f"xn{i}", [128, S, D]) for i in range(3)]
        xnT = [sb(f"xnT{i}", [128, S, B]) for i in range(3)]

        xbp = sb("xbp", [128, S, D])
        nscore = sb("nscore", [128, S, XH, B])
        nmax = sb("nmax", [128, S, XH])
        prob = sb("prob", [128, S, XH, B])
        psum_row = sb("psum_row", [128, S, XH])
        rsum = sb("rsum", [128, S, XH])
        probT = sb("probT", [128, S, XH, B])
        x1a = sb("x1a", [128, S, D])
        x1 = sb("x1", [128, S, D])
        x1b = sb("x1b", [128, S, D])

        qT = sb("qT", [128, S, B])
        kT = sb("kT", [128, S, B])
        v_sb = sb("v_sb", [128, S, D])
        qk = sb("qk", [128, S, S, B])
        sc = sb("sc", [128, S, S, H])
        scm = sb("scm", [128, S, H])
        scd = sb("scd", [128, S, S, H])
        pe_ = sb("pe_", [128, S, S, H])
        pes = sb("pes", [128, S, H])
        per = sb("per", [128, S, H])
        pn = sb("pn", [128, S, S, H])
        pv = sb("pv", [128, S, S, D])
        oT = sb("oT", [128, S, B])
        x2 = sb("x2", [128, S, D])
        x2b = sb("x2b", [128, S, D])

        hid = sb("hid", [128, 2, FC, S * B])
        acc = sb("acc", [128, 2, S, D])

        names = """x_in ctx_in wc_in ws_in small_in route_in ident_done ident_z mask_z mask_done
        sel_z sel_done tor_z tor_done half_done stats_done mv_done ve_done rstd_done xn_done xnT_ps xnT_done
        fold_ps fold_done kq_ps kq_done vp_ps vp_done wqkv_ps wqkv_done bqkv_ps bqkv_done bvw_done
        ob_ps ob_done xbp_done score_ps score_done exp_done rsum_done probT_ps probT_done
        xo_ps x1a_done x1_done x1b_done qv_ps k_ps q_done k_done v_done qk_done sc_ps sc_done
        scm_done scd_done pe_done pes_done per_done pn_done pv_done oT_ps oT_done so_ps x2_done
        x2b_done h_ps h_done y_ps acc_done idx_done iota_done pick_done pickw_done gate_done out_done""".split()
        s = {n: sem(n) for n in names}
        w1_in = [sem(f"w1_in{e}") for e in range(E // 2)]
        w2_in = [sem(f"w2_in{e}") for e in range(E // 2)]

        block = ctx.enter_context(nc.Block())

        @block.sync
        def _(sp):
            sp.dma_start(x_sb[:], x.rearrange("s b d -> b s d")).then_inc(s["x_in"], 16)
            sp.dma_start(ctx_sb[:], ctxT[:, :, 0:B]).then_inc(s["ctx_in"], 16)
            sp.dma_start(ws_sb[:], w_self).then_inc(s["ws_in"], 16)
            for p in range(E // 2):
                sp.dma_start(w1_sb[:, 2 * p:2 * p + 2], w1[:, 2 * p:2 * p + 2]).then_inc(w1_in[p], 16)
                sp.dma_start(w2_sb[:, 2 * p:2 * p + 2], w2[:, 2 * p:2 * p + 2]).then_inc(w2_in[p], 16)
            for t in range(S):
                sp.wait_ge(s["acc_done"], S * (E - 1) + t + 1)
                sp.dma_start(out[t], acc[:, (E - 1) % 2, t]).then_inc(s["out_done"], 16)
            sp.wait_ge(s["out_done"], 16 * S)

        @block.gpsimd
        def _(pool):
            g = nc.gpsimd
            g.memset(ident[:], 0.0).then_inc(s["ident_z"], 1)
            pool.wait_ge(s["ident_z"], 1)
            g.affine_select(out=ident[:], in_=ident[:], compare_op=ALU.not_equal, fill=1.0, base=0,
                            pattern=[[-1, 128]], channel_multiplier=1).then_inc(s["ident_done"], 1)
            g.memset(half[:], -0.5).then_inc(s["half_done"], 1)
            pool.wait_ge(s["half_done"], 1)
            pool.wait_ge(s["ve_done"], 1)
            g.tensor_tensor(rstd[0][:], var_eps[0][:], half[:], ALU.pow).then_inc(s["rstd_done"], 1)
            g.memset(mask[:], 0.0).then_inc(s["mask_z"], 1)
            pool.wait_ge(s["mask_z"], 1)
            g.affine_select(out=mask[:], in_=mask[:], compare_op=ALU.is_ge, fill=BIG, base=0,
                            pattern=[[0, XH], [-1, B]], channel_multiplier=1).then_inc(s["mask_done"], 1)
            pool.wait_ge(s["x_in"], 16)
            pool.wait_ge(s["small_in"], 32)
            g.tensor_tensor(xbp[:], x_sb[:], row_sb[:, 0, :].rearrange("p (o d) -> p o d", o=1).to_broadcast([128, S, D]),
                            ALU.add).then_inc(s["xbp_done"], 1)
            g.memset(head_sel[:], 1.0).then_inc(s["sel_z"], 1)
            pool.wait_ge(s["sel_z"], 1)
            g.affine_select(out=head_sel[:], in_=head_sel[:], compare_op=ALU.is_ge, fill=0.0, base=0,
                            pattern=[[-HD, H]], channel_multiplier=1).then_inc(s["sel_z"], 1)
            pool.wait_ge(s["sel_z"], 2)
            g.affine_select(out=head_sel[:], in_=head_sel[:], compare_op=ALU.is_ge, fill=0.0, base=HD - 1,
                            pattern=[[HD, H]], channel_multiplier=-1).then_inc(s["sel_done"], 1)
            g.memset(tor[:], 0.0).then_inc(s["tor_z"], 1)
            pool.wait_ge(s["tor_z"], 1)
            for i in range(S):
                for j in range(S):
                    n = (i == j) + ((i + 1) % S == j) + ((i - 1) % S == j)
                    if n:
                        g.memset(tor[:, i, j:j + 1], float(n)).then_inc(s["tor_done"], 1)
            g.iota(iota_e[:], pattern=[[1, E]], base=0, channel_multiplier=0,
                   allow_small_or_imprecise_dtypes=True).then_inc(s["iota_done"], 1)
            pool.wait_ge(s["route_in"], 32)
            g.tensor_copy(idx_f[:], idx_sb[:]).then_inc(s["idx_done"], 1)
            pool.wait_ge(s["pick_done"], TOPK)
            for j in range(TOPK):
                g.tensor_tensor(pick_w[:, j], pick[:, j], wt_sb[:, :, j:j + 1].to_broadcast([128, S, E]), ALU.mult).then_inc(s["pickw_done"], 1)
            pool.wait_ge(s["pickw_done"], TOPK)
            g.tensor_tensor(gate[:], pick_w[:, 0], pick_w[:, 1], ALU.add).then_inc(s["gate_done"], 1)
            for t in range(S):
                pool.wait_ge(s["ve_done"], 2 + t)
                g.tensor_tensor(rstd[1][:, t:t + 1], var_eps[1][:, t:t + 1], half[:, 0:1], ALU.pow).then_inc(s["rstd_done"], 1)
            pool.wait_ge(s["ob_done"], 1)
            g.tensor_tensor(x1b[:], x1[:], out_bias[:].rearrange("p (o d) -> p o d", o=1).to_broadcast([128, S, D]),
                            ALU.add).then_inc(s["x1b_done"], 1)
            for t in range(S):
                pool.wait_ge(s["ve_done"], 2 + S + t)
                g.tensor_tensor(rstd[2][:, t:t + 1], var_eps[2][:, t:t + 1], half[:, 0:1], ALU.pow).then_inc(s["rstd_done"], 1)
            g.tensor_tensor(x2b[:], x2[:], row_sb[:, 2, :].rearrange("p (o d) -> p o d", o=1).to_broadcast([128, S, D]),
                            ALU.add).then_inc(s["x2b_done"], 1)

        @block.scalar
        def _(act):
            a = nc.scalar
            act.dma_start(wc_sb[:], w_cross).then_inc(s["wc_in"], 16)
            act.dma_start(row_sb[:], rows.rearrange("(o r) d -> o r d", o=1).to_broadcast([128, 3, D])).then_inc(s["small_in"], 16)
            act.dma_start(col_sb[:], cols).then_inc(s["small_in"], 16)
            act.dma_start(idx_sb[:], exp_idx).then_inc(s["route_in"], 16)
            act.dma_start(wt_sb[:], exp_wt).then_inc(s["route_in"], 16)
            a.preload_act_table(ACT.Exp)
            for n in range(2):
                for h in range(XH):
                    act.wait_ge(s["fold_ps"], 2 * XH)
                    a.activation(fold_sb[:, n, h], bank[FOLD_BANK[h]][:, n * D:(n + 1) * D], ACT.Copy).then_inc(s["fold_done"], 1)
            act.wait_ge(s["kq_ps"], 1)
            a.activation(kq_sb[:, :, 0, :], bank[KQ_BANK[0]][:].rearrange("p (s k) -> p s k", s=S), ACT.Copy,
                         scale=-float(DK) ** -0.5).then_inc(s["kq_done"], 1)
            act.wait_ge(s["wqkv_ps"], 1)
            a.activation(wqkv_sb[:].rearrange("p a d -> p (a d)"), bank[WQKV_BANK][:, 0:3 * D], ACT.Copy).then_inc(s["wqkv_done"], 1)
            for p in range(2):
                act.wait_ge(s["vp_ps"], p + 1)
                a.activation(vp_sb[:, 2 * p:2 * p + 2].rearrange("p s h d -> p (s h d)"), bank[VP_BANK[p]][:], ACT.Copy).then_inc(s["vp_done"], 1)
            for t in range(S):
                for h in range(XH):
                    act.wait_ge(s["score_done"], XH * t + h + 1)
                    a.activation(prob[:, t, h], nscore[:, t, h], ACT.Exp, bias=nmax[:, t, h:h + 1], scale=-1.0,
                                 accum_out=psum_row[:, t, h:h + 1]).then_inc(s["exp_done"], 1)
                if t >= 1:
                    act.wait_ge(s["probT_ps"], t)
                    a.activation(probT[:, t - 1].rearrange("p h k -> p (h k)"),
                                 bank[PROBT_BANK[t - 1]][:, 0:XH * B], ACT.Copy).then_inc(s["probT_done"], 1)
            t = S - 1
            act.wait_ge(s["probT_ps"], S)
            a.activation(probT[:, t].rearrange("p h k -> p (h k)"), bank[PROBT_BANK[t]][:, 0:XH * B],
                         ACT.Copy).then_inc(s["probT_done"], 1)
            act.wait_ge(s["bqkv_done"], 2)
            for t in range(S):
                act.wait_ge(s["xnT_ps"], S + t + 1)
                a.activation(xnT[1][:, t], bank[XNT1_BANK[t]][:, 0:B], ACT.Copy).then_inc(s["xnT_done"], 1)
                act.wait_ge(s["qv_ps"], t + 1)
                a.activation(qT[:, t], bank[QV_BANK[t]][:, 0:B], ACT.Identity, bias=bq_scaled[:, 0:1],
                             scale=float(HD) ** -0.5).then_inc(s["q_done"], 1)
            for t in range(S):
                a.activation(v_sb[:, t], bank[QV_BANK[t]][:, B:B + D], ACT.Copy).then_inc(s["v_done"], 1)
            act.wait_ge(s["scd_done"], 1)
            a.activation(pe_[:].rearrange("p q k h -> p (q k h)"), scd[:].rearrange("p q k h -> p (q k h)"), ACT.Exp).then_inc(s["pe_done"], 1)
            a.preload_act_table(ACT.Gelu)
            for t in range(S):
                act.wait_ge(s["oT_ps"], t + 1)
                a.activation(oT[:, t], bank[OT_BANK[t]][:, 0:B], ACT.Copy).then_inc(s["oT_done"], 1)
            for t in range(S):
                act.wait_ge(s["xnT_ps"], 2 * S + t + 1)
                a.activation(xnT[2][:, t], bank[XNT2_BANK[t]][:, 0:B], ACT.Copy).then_inc(s["xnT_done"], 1)
            for e in range(E):
                if e >= 2:
                    act.wait_ge(s["y_ps"], S * (e - 1))
                for c in range(FC):
                    act.wait_ge(s["h_ps"], FC * e + c + 1)
                    a.activation(hid[:, e % 2, c], bank[H_BANK[c]][:], ACT.Gelu).then_inc(s["h_done"], 1)

        @block.vector
        def _(dve):
            v = nc.vector

            def normalise(n, t, done_stats, done_mv, ve):
                dve.wait_ge(s["stats_done"], done_stats)
                v.bn_aggr(mv[n][:, t], stats[n][:, t]).then_inc(s["mv_done"], 1)

            dve.wait_ge(s["x_in"], 16)
            for t in range(S):
                v.bn_stats(stats[0][:, t], x_sb[:, t]).then_inc(s["stats_done"], 1)
            for t in range(S):
                normalise(0, t, t + 1, None, None)
            dve.wait_ge(s["mv_done"], S)
            v.tensor_scalar(var_eps[0][:], mv[0][:, :, 1], EPS, None, ALU.add).then_inc(s["ve_done"], 1)
            dve.wait_ge(s["rstd_done"], 1)
            for t in range(S):
                v.tensor_scalar(xn[0][:, t], x_sb[:, t], mv[0][:, t, 0:1], rstd[0][:, t:t + 1], ALU.subtract,
                                ALU.mult).then_inc(s["xn_done"], 1)
            dve.wait_ge(s["idx_done"], 1)
            dve.wait_ge(s["iota_done"], 1)
            for j in range(TOPK):
                v.tensor_tensor(pick[:, j], idx_f[:, :, j:j + 1].to_broadcast([128, S, E]),
                                iota_e[:].rearrange("p (o e) -> p o e", o=1).to_broadcast([128, S, E]),
                                ALU.is_equal).then_inc(s["pick_done"], 1)
            dve.wait_ge(s["xnT_ps"], S)
            v.tensor_copy(xnT[0][:].rearrange("p s b -> p (s b)"), bank[XNT_BANK][:]).then_inc(s["xnT_done"], 1)
            dve.wait_ge(s["kq_ps"], 2)
            v.tensor_scalar(kq_sb[:, :, 1, :], bank[KQ_BANK[1]][:].rearrange("p (s k) -> p s k", s=S), -float(DK) ** -0.5, None,
                            ALU.mult).then_inc(s["kq_done"], 1)
            dve.wait_ge(s["mask_done"], 1)
            for t in range(S):
                dve.wait_ge(s["score_ps"], t + 1)
                for h in range(XH):
                    v.tensor_tensor_reduce(out=nscore[:, t, h], in0=bank[SCORE_BANK[t]][:, h * B:(h + 1) * B], in1=mask[:, h],
                                           scale=1.0, scalar=3.0e38, op0=ALU.add, op1=ALU.min,
                                           accum_out=nmax[:, t, h:h + 1]).then_inc(s["score_done"], 1)
            dve.wait_ge(s["small_in"], 32)
            dve.wait_ge(s["bqkv_ps"], 1)
            v.tensor_tensor(bqkv[:], bank[WQKV_BANK][:, 384:387], col_sb[:, 1:4], ALU.add).then_inc(s["bqkv_done"], 1)
            dve.wait_ge(s["bqkv_done"], 1)
            v.tensor_scalar(bq_scaled[:], bqkv[:, 0:1], float(HD) ** -0.5, None, ALU.mult).then_inc(s["bqkv_done"], 1)
            v.tensor_copy(bv_wide[:], bqkv[:, 2:3].to_broadcast([128, 128])).then_inc(s["bvw_done"], 1)
            dve.wait_ge(s["xbp_done"], 1)
            for t in range(S):
                dve.wait_ge(s["exp_done"], XH * (t + 1))
                v.reciprocal(rsum[:, t], psum_row[:, t]).then_inc(s["rsum_done"], 1)
                dve.wait_ge(s["rsum_done"], t + 1)
                dve.wait_ge(s["xo_ps"], t + 1)
                v.scalar_tensor_tensor(out=x1a[:, t], in0=bank[XO_BANK[t]][:, 0:D], scalar=rsum[:, t, 0:1], in1=xbp[:, t],
                                       op0=ALU.mult, op1=ALU.add).then_inc(s["x1a_done"], 1)
                dve.wait_ge(s["x1a_done"], t + 1)
                v.scalar_tensor_tensor(out=x1[:, t], in0=bank[XO_BANK[t]][:, D:2 * D], scalar=rsum[:, t, 1:2],
                                       in1=x1a[:, t], op0=ALU.mult, op1=ALU.add).then_inc(s["x1_done"], 1)
                dve.wait_ge(s["x1_done"], t + 1)
                v.bn_stats(stats[1][:, t], x1[:, t]).then_inc(s["stats_done"], 1)
                normalise(1, t, S + t + 1, None, None)
                dve.wait_ge(s["mv_done"], S + t + 1)
                v.tensor_scalar(var_eps[1][:, t:t + 1], mv[1][:, t, 1:2], EPS, None, ALU.add).then_inc(s["ve_done"], 1)
                dve.wait_ge(s["rstd_done"], 2 + t)
                v.tensor_scalar(xn[1][:, t], x1[:, t], mv[1][:, t, 0:1], rstd[1][:, t:t + 1], ALU.subtract,
                                ALU.mult).then_inc(s["xn_done"], 1)
            dve.wait_ge(s["ob_ps"], 1)
            v.tensor_tensor(out_bias[:], bank[OB_BANK][:, 0:D], row_sb[:, 1, :], ALU.add).then_inc(s["ob_done"], 1)
            for p in range(2):
                dve.wait_ge(s["k_ps"], p + 1)
                v.tensor_scalar(kT[:, 2 * p:2 * p + 2].rearrange("p s b -> p (s b)"), bank[K_BANK[p]][:, 0:2 * B], bqkv[:, 1:2], None, ALU.add).then_inc(s["k_done"], 1)
            dve.wait_ge(s["k_done"], 2)
            for q in range(S):
                dve.wait_ge(s["q_done"], q + 1)
                v.tensor_tensor(qk[:, q], qT[:, q].rearrange("p (o b) -> p o b", o=1).to_broadcast([128, S, B]), kT[:],
                                ALU.mult).then_inc(s["qk_done"], 1)
            dve.wait_ge(s["tor_done"], 3 * S)
            dve.wait_ge(s["sc_ps"], 1)
            v.tensor_tensor(sc[:].rearrange("p q k h -> p (q k) h"), bank[SC_BANK][:, 0:S * S * H].rearrange("p (a h) -> p a h", h=H),
                            tor[:].rearrange("p q (k o) -> p (q k) o", o=1).to_broadcast([128, S * S, H]), ALU.add).then_inc(s["sc_done"], 1)
            dve.wait_ge(s["sc_done"], 1)
            v.tensor_reduce(scm[:], sc[:].rearrange("p q k h -> p q h k"), AX.X, ALU.max).then_inc(s["scm_done"], 1)
            dve.wait_ge(s["scm_done"], 1)
            v.tensor_tensor(scd[:], sc[:], scm[:].rearrange("p q (o h) -> p q o h", o=1).to_broadcast([128, S, S, H]),
                            ALU.subtract).then_inc(s["scd_done"], 1)
            dve.wait_ge(s["pe_done"], 1)
            v.tensor_reduce(pes[:], pe_[:].rearrange("p q k h -> p q h k"), AX.X, ALU.add).then_inc(s["pes_done"], 1)
            dve.wait_ge(s["pes_done"], 1)
            v.reciprocal(per[:], pes[:]).then_inc(s["per_done"], 1)
            dve.wait_ge(s["per_done"], 1)
            v.tensor_tensor(pn[:], pe_[:], per[:].rearrange("p q (o h) -> p q o h", o=1).to_broadcast([128, S, S, H]),
                            ALU.mult).then_inc(s["pn_done"], 1)
            dve.wait_ge(s["pn_done"], 1)
            dve.wait_ge(s["v_done"], S)
            for q in range(S):
                v.tensor_tensor(pv[:, q].rearrange("p k (h d) -> p (k h) d", d=HD),
                                pn[:, q].rearrange("p k (h o) -> p (k h) o", o=1).to_broadcast([128, S * H, HD]),
                                v_sb[:].rearrange("p k (h d) -> p (k h) d", d=HD), ALU.mult).then_inc(s["pv_done"], 1)
            dve.wait_ge(s["x1b_done"], 1)
            for t in range(S):
                dve.wait_ge(s["so_ps"], t + 1)
                v.tensor_tensor(x2[:, t], bank[SO_BANK[t]][:, 0:D], x1b[:, t], ALU.add).then_inc(s["x2_done"], 1)
                dve.wait_ge(s["x2_done"], t + 1)
                v.bn_stats(stats[2][:, t], x2[:, t]).then_inc(s["stats_done"], 1)
                normalise(2, t, 2 * S + t + 1, None, None)
                dve.wait_ge(s["mv_done"], 2 * S + t + 1)
                v.tensor_scalar(var_eps[2][:, t:t + 1], mv[2][:, t, 1:2], EPS, None, ALU.add).then_inc(s["ve_done"], 1)
                dve.wait_ge(s["rstd_done"], 2 + S + t)
                v.tensor_scalar(xn[2][:, t], x2[:, t], mv[2][:, t, 0:1], rstd[2][:, t:t + 1], ALU.subtract,
                                ALU.mult).then_inc(s["xn_done"], 1)
            dve.wait_ge(s["gate_done"], 1)
            dve.wait_ge(s["x2b_done"], 1)
            for e in range(E):
                for t in range(S):
                    dve.wait_ge(s["y_ps"], S * e + t + 1)
                    if e:
                        dve.wait_ge(s["acc_done"], S * (e - 1) + t + 1)
                    v.scalar_tensor_tensor(out=acc[:, e % 2, t], in0=bank[Y_BANK[t]][:, 0:D],
                                           scalar=gate[:, t, e:e + 1], in1=acc[:, (e - 1) % 2, t] if e else x2b[:, t],
                                           op0=ALU.mult, op1=ALU.add).then_inc(s["acc_done"], 1)

        @block.tensor
        def _(pe):
            mm, tr = nc.tensor.matmul, nc.tensor.transpose
            pe.wait_ge(s["wc_in"], 16)
            for n in range(2):
                for h in range(XH):
                    r = slice(h * DK, (h + 1) * DK)
                    mm(bank[FOLD_BANK[h]][:, n * D:(n + 1) * D], wc_sb[r, 1 + n, :], wc_sb[r, 3 * n, :],
                       start=True, stop=True).then_inc(s["fold_ps"], 1)
            pe.wait_ge(s["ident_done"], 1)
            for t in range(S):
                pe.wait_ge(s["xn_done"], t + 1)
                tr(bank[XNT_BANK][:, t * B:(t + 1) * B], xn[0][:, t], ident[:]).then_inc(s["xnT_ps"], 1)
            pe.wait_ge(s["ctx_in"], 16)
            for h in range(XH):
                pe.wait_ge(s["fold_done"], h + 1)
                mm(bank[KQ_BANK[h]][:], fold_sb[:, 0, h], ctx_sb[:].rearrange("p s k -> p (s k)"), start=True, stop=True).then_inc(s["kq_ps"], 1)
            pe.wait_ge(s["ws_in"], 16)
            mm(bank[WQKV_BANK][:, 0:3 * D], ws_sb[:, 0], ws_sb[:, 1:4].rearrange("p a d -> p (a d)"), start=True, stop=True).then_inc(s["wqkv_ps"], 1)
            pe.wait_ge(s["kq_done"], 2)
            pe.wait_ge(s["xnT_done"], 1)
            for t in range(S):
                mm(bank[SCORE_BANK[t]][:, 0:XH * B], xnT[0][:, t], kq_sb[:, t].rearrange("p h k -> p (h k)"),
                   start=True, stop=True).then_inc(s["score_ps"], 1)
            pe.wait_ge(s["fold_done"], 2 * XH)
            for t in range(S):
                last = mm(bank[VP_BANK[t // 2]][:, t % 2 * 256:t % 2 * 256 + 256], ctx_sb[:, t], fold_sb[:, 1].rearrange("p h d -> p (h d)"),
                          start=True, stop=True)
                if t % 2:
                    last.then_inc(s["vp_ps"], 1)
            pe.wait_ge(s["small_in"], 32)
            pe.wait_ge(s["wqkv_done"], 1)
            for a in range(3):
                last = mm(bank[WQKV_BANK][:, 384 + a:385 + a], ws_sb[:, 1 + a], col_sb[:, 0:1], start=True, stop=True)
            last.then_inc(s["bqkv_ps"], 1)

            def probs_out(t):
                pe.wait_ge(s["probT_done"], t + 1)
                pe.wait_ge(s["vp_done"], 2)
                if t == 2:
                    pe.wait_ge(s["score_done"], XH * S)
                for h in range(XH):
                    last = mm(bank[XO_BANK[t]][:, h * D:(h + 1) * D], probT[:, t, h], vp_sb[:, t, h], start=True, stop=True)
                last.then_inc(s["xo_ps"], 1)

            for t in range(S):
                for h in range(XH):
                    pe.wait_ge(s["exp_done"], XH * t + h + 1)
                    last = tr(bank[PROBT_BANK[t]][:, h * B:(h + 1) * B], prob[:, t, h], ident[:])
                last.then_inc(s["probT_ps"], 1)
                if t:
                    probs_out(t - 1)
            probs_out(S - 1)

            def project(t):
                pe.wait_ge(s["xnT_done"], 1 + t + 1)
                mm(bank[QV_BANK[t]][:, 0:B], wqkv_sb[:, 0], xnT[1][:, t], start=True, stop=True)
                mm(bank[QV_BANK[t]][:, B:B + D], xnT[1][:, t], wqkv_sb[:, 2], start=True, stop=True).then_inc(s["qv_ps"], 1)
                last = mm(bank[K_BANK[t // 2]][:, t % 2 * B:t % 2 * B + B], wqkv_sb[:, 1], xnT[1][:, t], start=True, stop=True)
                if t % 2:
                    last.then_inc(s["k_ps"], 1)

            pe.wait_ge(s["bqkv_done"], 1)
            for t in range(S):
                pe.wait_ge(s["xn_done"], S + t + 1)
                tr(bank[XNT1_BANK[t]][:, 0:B], xn[1][:, t], ident[:]).then_inc(s["xnT_ps"], 1)
                if t:
                    project(t - 1)
            pe.wait_ge(s["bvw_done"], 1)
            pe.wait_ge(s["x1_done"], S)
            mm(bank[OB_BANK][:, 0:D], bv_wide[:], ws_sb[:, 4], start=True, stop=True).then_inc(s["ob_ps"], 1)
            project(S - 1)
            pe.wait_ge(s["sel_done"], 1)
            for q in range(S):
                pe.wait_ge(s["qk_done"], q + 1)
                for k in range(S):
                    o = (q * S + k) * H
                    last = mm(bank[SC_BANK][:, o:o + H], qk[:, q, k], head_sel[:], start=True, stop=True)
            last.then_inc(s["sc_ps"], 1)
            pe.wait_ge(s["ob_done"], 1)
            pe.wait_ge(s["sc_done"], 1)
            pe.wait_ge(s["q_done"], S)
            pe.wait_ge(s["k_done"], 2)
            pe.wait_ge(s["v_done"], S)
            for q in range(S):
                pe.wait_ge(s["pv_done"], q + 1)
                for k in range(S):
                    last = mm(bank[OT_BANK[q]][:, 0:B], pv[:, q, k], ident[:], start=(k == 0), stop=(k == S - 1))
                last.then_inc(s["oT_ps"], 1)
                if q:
                    pe.wait_ge(s["oT_done"], q)
                    mm(bank[SO_BANK[q - 1]][:, 0:D], oT[:, q - 1], ws_sb[:, 4], start=True, stop=True).then_inc(s["so_ps"], 1)
            pe.wait_ge(s["oT_done"], S)
            mm(bank[SO_BANK[S - 1]][:, 0:D], oT[:, S - 1], ws_sb[:, 4], start=True, stop=True).then_inc(s["so_ps"], 1)
            for t in range(S):
                pe.wait_ge(s["xn_done"], 2 * S + t + 1)
                tr(bank[XNT2_BANK[t]][:, 0:B], xn[2][:, t], ident[:]).then_inc(s["xnT_ps"], 1)
            pe.wait_ge(s["xnT_done"], 1 + 2 * S)
            pe.wait_ge(s["x2_done"], S)

            def hidden(e):
                pe.wait_ge(w1_in[e // 2], 16)
                for c in range(FC):
                    if e:
                        pe.wait_ge(s["h_done"], FC * (e - 1) + c + 1)
                    mm(bank[H_BANK[c]][:], w1_sb[:, e, c * 128:(c + 1) * 128], xnT[2][:].rearrange("p s b -> p (s b)"),
                       start=True, stop=True).then_inc(s["h_ps"], 1)

            def expert_out(e):
                pe.wait_ge(w2_in[e // 2], 16)
                pe.wait_ge(s["h_done"], FC * (e + 1))
                for t in range(S):
                    if e:
                        pe.wait_ge(s["acc_done"], S * (e - 1) + t + 1)
                    for c in range(FC):
                        last = mm(bank[Y_BANK[t]][:, 0:D], hid[:, e % 2, c, t * B:(t + 1) * B], w2_sb[:, e, c],
                                  start=(c == 0), stop=(c == FC - 1))
                    last.then_inc(s["y_ps"], 1)

            for e in range(E):
                hidden(e)
                if e:
                    expert_out(e - 1)
            expert_out(E - 1)


_ORDER = ["x", "ctxT", "w_cross", "w_self", "cols", "rows", "exp_idx", "exp_wt", "w1", "w2"]


def kernel(x, ctx_1024, L0_xattn_Wq, L0_xattn_Wk, L0_xattn_Wv, L0_xattn_Wp, L0_xattn_bp, L0_attn_w_tor, L0_attn_b_tor,
           L0_attn_in_proj_w, L0_attn_in_proj_b, L0_attn_out_w, L0_attn_out_b, L0_ffn_scores, L0_ffn_expert_weights,
           L0_ffn_expert_indices, L0_ffn_w1, L0_ffn_w2, L0_ffn_bias):
    import numpy as np
    import concourse.bacc as bacc
    from concourse import mybir as _mybir
    from concourse.bass_utils import run_bass_kernel_spmd

    A = np.asarray
    c = np.ascontiguousarray
    S, B, D = A(x).shape
    E, _, FF = A(L0_ffn_w1).shape
    ipw = A(L0_attn_in_proj_w)
    arrays = {
        "x": c(A(x)),
        "ctxT": c(A(ctx_1024).transpose(2, 0, 1)),
        "w_cross": c(np.stack([A(L0_xattn_Wq), A(L0_xattn_Wk), A(L0_xattn_Wv), A(L0_xattn_Wp).T], axis=1)),
        "w_self": c(np.concatenate([A(L0_attn_w_tor), ipw.T, A(L0_attn_out_w).T], axis=1).reshape(D, 5, D)),
        "cols": c(np.concatenate([A(L0_attn_b_tor).reshape(D, 1), A(L0_attn_in_proj_b).reshape(3, D).T], axis=1)),
        "rows": c(np.stack([A(L0_xattn_bp), A(L0_attn_out_b), A(L0_ffn_bias)])),
        "exp_idx": c(A(L0_ffn_expert_indices).reshape(S, B, -1).transpose(1, 0, 2)),
        "exp_wt": c(A(L0_ffn_expert_weights).reshape(S, B, -1).transpose(1, 0, 2)),
        "w1": c(A(L0_ffn_w1).transpose(1, 0, 2)),
        "w2": c(A(L0_ffn_w2).reshape(E, FF // 128, 128, D).transpose(2, 0, 1, 3)),
    }
    nc = bacc.Bacc("TRN2", target_bir_lowering=False, num_devices=1)
    args = [nc.dram_tensor(f"in_{n}", arrays[n].shape, _mybir.dt.from_np(arrays[n].dtype), kind="ExternalInput").ap()
            for n in _ORDER]
    out = nc.dram_tensor("out_0", (S, B, D), _mybir.dt.float32, kind="ExternalOutput").ap()
    perceiver_layer(nc, *args, out)
    r = run_bass_kernel_spmd(nc, [{f"in_{n}": arrays[n] for n in _ORDER}], core_ids=[0])
    return r.results[0]["out_0"]
```

```python
from contextlib import ExitStack

import concourse.bass as bass
from concourse import mybir

ALU = mybir.AluOpType
ACT = mybir.ActivationFunctionType
AX = mybir.AxisListType
F32 = mybir.dt.float32
I32 = mybir.dt.int32
BF16 = mybir.dt.bfloat16


def perceiver_layer(nc, x, ctxT, w_cross, w_self, cols, in_bias, rows, exp_idx, exp_wt, w1, w2, out):
    S, B, D = x.shape
    XH, DK = 2, D // 2
    H, HD = 16, D // 16
    E, FF = w1.shape[1:]
    FC = FF // 128
    TOPK = 2
    UNPAIRED = 2
    QSCALE = float(HD) ** -0.5
    CHUNK = 128
    CAP = CHUNK + CHUNK // E
    SLOTS = E * CAP
    LIMIT = CAP
    SC = SLOTS // CHUNK
    CODE = 4096.0
    BIG = 1.0e13
    EPS = 1e-5
    FOLD_BANK = [0, 3]
    KQ_BANK = [1, 2]
    XNT_BANK = 5
    WQKV_BANK = 4
    BQKV_BANK = 7
    VP_BANK = [0, 3]
    SCORE_BANK = [6, 5, 1, 2]
    PROBT_BANK = SCORE_BANK
    XO_BANK = [0, 3, 6, 5]
    XNT1_BANK = [1, 2, 0, 3]
    QKV_BANK = [4, 7, 1, 6]
    OT_BANK = [2, 3, 4, 5]
    SO_BANK = [6, 1, 2, 3]
    RANK_BANK = 7
    TURN_BANK = [7, 0]
    GATE_BANK = 6
    GATHER_BANK = [0, 4, 5]
    HR_BANK = [6, 1]
    YT_BANK = 7
    YS_BANK = [2] * (SC - 1) + [6]
    SUM_BANK = [0, 4, 5, 3]
    XNT2_BANK = [0, 3, 4, 6]
    WARM_BANK = 7
    H_BANK = [7, 5, 1, 2]
    Y_BANK = [0, 3, 4, 6]
    TURNS = 6
    W0, W1, W2, W3, W4, W5 = [512, 512, 64], 0, 0, 1, 4, 1

    def last_expert(k):
        return min(k, E - 1)

    with ExitStack() as ctx:
        def sb(name, shape, dt=F32):
            return ctx.enter_context(nc.sbuf_tensor(name, shape, dt))

        def sem(name):
            return ctx.enter_context(nc.semaphore(name))

        bank = [ctx.enter_context(nc.psum_tensor(f"bank{i}", [128, 512], F32)) for i in range(8)]

        x_sb = sb("x_sb", [128, S, D])
        ctx_sb = sb("ctx_sb", [128, S, B])
        wc_sb = sb("wc_sb", [128, 4, D])
        ws_sb = sb("ws_sb", [128, 5, D])
        btor_sb = sb("btor_sb", [128, 1])
        row_sb = sb("row_sb", [128, 3, D])
        idx_sb = sb("idx_sb", [128, S, TOPK], I32)
        wt_sb = sb("wt_sb", [128, S, TOPK])
        w1_sb = sb("w1_sb", [128, E, FF])
        w2_sb = sb("w2_sb", [128, E, FC, D])

        ident = sb("ident", [128, 128])
        mask = sb("mask", [128, XH, B])
        tor = sb("tor", [128, S, S])
        half = sb("half", [128, S])

        fold_sb = sb("fold_sb", [128, 2, XH, D])
        kq_sb = sb("kq_sb", [128, S, XH, B])
        vp_sb = sb("vp_sb", [128, S, XH, D])
        wqkv_sb = sb("wqkv_sb", [128, 3, D])
        bqkv = sb("bqkv", [128, 3 * D])
        ones = sb("ones", [128, 128])
        warm = sb("warm", [128, 512], mybir.dt.bfloat16)
        gate = sb("gate", [128, S, E])
        iota_e = sb("iota_e", [128, E])
        idx_f = sb("idx_f", [128, S, TOPK])
        pick = sb("pick", [128, TOPK, S, E])
        pick_w = sb("pick_w", [128, TOPK, S, E])

        stats = [sb(f"stats{i}", [128, S, 6]) for i in range(3)]
        mv = [sb(f"mv{i}", [128, S, 2]) for i in range(3)]
        var_eps = [sb(f"var_eps{i}", [128, S]) for i in range(3)]
        rstd = [sb(f"rstd{i}", [128, S]) for i in range(3)]
        xn = [sb(f"xn{i}", [128, S, D]) for i in range(3)]
        xnT = [sb(f"xnT{i}", [128, S, B]) for i in range(3)]

        xbp = sb("xbp", [128, S, D])
        nscore = sb("nscore", [128, S, XH, B])
        nmax = sb("nmax", [128, S, XH])
        prob = sb("prob", [128, S, XH, B])
        psum_row = sb("psum_row", [128, S, XH])
        rsum = sb("rsum", [128, S, XH])
        probT = sb("probT", [128, S, XH, B])
        x1a = sb("x1a", [128, S, D])
        x1 = sb("x1", [128, S, D])
        x1b = sb("x1b", [128, S, D])

        qkv = sb("qkv", [128, S, 3, D])
        qk = sb("qk", [128, S, S, D])
        sc0 = sb("sc0", [128, S, S, H])
        sc = sb("sc", [128, S, S, H])
        scm = sb("scm", [128, S, H])
        scd = sb("scd", [128, S, S, H])
        expd = sb("expd", [128, S, S, H])
        exps = sb("exps", [128, S, H])
        expr = sb("expr", [128, S, H])
        pn = sb("pn", [128, S, S, H])
        pv = sb("pv", [128, S, S, D])
        pv2 = sb("pv2", [128, S, S // 2, D])
        oT = sb("oT", [128, S, B])
        x2 = sb("x2", [128, S, D])
        x2b = sb("x2b", [128, S, D])

        tri_b = sb("tri_b", [128, 128], BF16)
        ones_b = sb("ones_b", [128, 128], BF16)
        ident_b = sb("ident_b", [128, 128], BF16)
        picked = sb("picked", [128, S + 1, E], BF16)
        code0 = sb("code0", [128, S, E])
        code = sb("code", [128, S, E], BF16)
        most = sb("most", [128, 1], I32)
        slot_no = sb("slot_no", [128, CAP, E], BF16)
        take = sb("take", [128, S, CAP, E], BF16)
        takeT = sb("takeT", [128, SC, S * B], BF16)
        owner = sb("owner", [128, E])
        gate3 = sb("gate3", [128, S, 3, E], BF16)
        gate_r = sb("gate_r", [128, 2, S, E])
        shared = sb("shared", [128, 3, E])
        slot_gate = sb("slot_gate", [128, SC])
        xn3 = sb("xn3", [128, S, 3, D], BF16)
        xn3_r = sb("xn3_r", [128, S, D])
        ysr = sb("ysr", [128, 2, D])
        xg = sb("xg", [128, SLOTS])
        yT = sb("yT", [128, CAP, E])
        ys = sb("ys", [128, 2, D])
        ys3 = sb("ys3", [128, 2, 3, D], BF16)

        hid = sb("hid", [128, 2, FC, S * B])
        acc = sb("acc", [128, 2, S, D])
        hidr = hid[:, :, :, 0:CAP]
        res = acc[:, 0]

        names = """x_in ctx_in wc_in ws_in rows_in bias_in route_in warm_done ones_done bqkv_z ident_done ident_z
        mask_z mask_done tor_z tor_done half_done stats_done mv_done ve_done rstd_done xn_done xnT_ps xnT0_done xnT_done
        fold_ps fold_done kq_ps kq_done vp_ps vp_done vp_done1 wqkv_ps wqkv_done bqkv_ps bqkv_done
        xbp_done score_ps score_done exp_done rsum_done probT_ps probT_done xo_ps x1a_done x1_done x1b_done
        qkv_ps qkv_done qk_done qk_pool sc0_done sc_done scm_done scd_done expd_done exps_done expr_done pn_done
        pv_done pv_pool pv2_done oT_ps oT_done so_ps x2_done x2b_done h_ps h_done y_ps acc_done
        picked_z picked_done tri_done onesb_done identb_done gatehi_done gater_done gatemid_done gater2_done gate3_done split_hi split_r split_mid split_lo yshi_done ysr_done ysmid_done yslo_done rank_ps most_ps code_done most_done slot_done take_done owner_z owner_done sgate_ps sgates_done sgate_done turn_ps turn_done
        xg_ps xg_done xg_act hr_ps hr_done yT_ps yT_done ys_ps ys_done scatter_done sum_ps res_done outr_done
        idx_done iota_done pick_done pickw_done gate_done out_done""".split()
        s = {n: sem(n) for n in names}
        w1_in = [sem(f"w1_in{e}") for e in range(E // 2)]
        w2_in = [sem(f"w2_in{e}") for e in range(E // 2)]

        block = ctx.enter_context(nc.Block())

        @block.sync
        def _(sp):
            sp.dma_start(x_sb[:], x.rearrange("s b d -> b s d")).then_inc(s["x_in"], 16)
            sp.dma_start(ctx_sb[:], ctxT[:, :, 0:B]).then_inc(s["ctx_in"], 16)
            sp.dma_start(ws_sb[:], w_self).then_inc(s["ws_in"], 16)
            sp.dma_start(idx_sb[:], exp_idx).then_inc(s["route_in"], 16)
            sp.dma_start(wt_sb[:], exp_wt).then_inc(s["route_in"], 16)
            sp.dma_start(btor_sb[:], cols).then_inc(s["bias_in"], 16)
            sp.wait_ge(s["bqkv_z"], 1)
            sp.dma_start(bqkv[32:33, :], in_bias).then_inc(s["bias_in"], 16)
            sp.dma_start(row_sb[:], rows.rearrange("(o r) d -> o r d", o=1).to_broadcast([128, 3, D])).then_inc(s["rows_in"], 16)
            for p in range(E // 2):
                sp.dma_start(w1_sb[:, 2 * p:2 * p + 2], w1[:, 2 * p:2 * p + 2]).then_inc(w1_in[p], 16)
                sp.dma_start(w2_sb[:, 2 * p:2 * p + 2], w2[:, 2 * p:2 * p + 2]).then_inc(w2_in[p], 16)
            sp.wait_ge(s["most_done"], 1)
            fullest = sp.alloc_register("fullest_for_sp")
            sp.reg_load(fullest, most[0:1, 0:1])
            with sp.If_lt(fullest, LIMIT + 1):
                for t in (0, 2):
                    sp.wait_ge(s["res_done"], t + 2)
                    sp.dma_start(out[t:t + 2].rearrange("s b d -> b s d"), res[:, t:t + 2]).then_inc(s["out_done"], 32)
            with sp.Else():
                for t in range(S):
                    sp.wait_ge(s["acc_done"], S * (E - 1) + t + 1)
                    sp.dma_start(out[t], acc[:, (E - 1) % 2, t]).then_inc(s["out_done"], 16)
            sp.wait_ge(s["out_done"], 16 * S)

        @block.gpsimd
        def _(pool):
            g = nc.gpsimd
            g.memset(bqkv[:], 0.0).then_inc(s["bqkv_z"], 1)
            g.memset(ident[:], 0.0).then_inc(s["ident_z"], 1)
            pool.wait_ge(s["ident_z"], 1)
            g.affine_select(out=ident[:], in_=ident[:], compare_op=ALU.not_equal, fill=1.0, base=0,
                            pattern=[[-1, 128]], channel_multiplier=1).then_inc(s["ident_done"], 1)
            g.memset(ones[:], 1.0).then_inc(s["ones_done"], 1)
            pool.wait_ge(s["ident_done"], 1)
            g.tensor_copy(ident_b[:], ident[:]).then_inc(s["identb_done"], 1)
            g.memset(half[:], -0.5).then_inc(s["half_done"], 1)
            g.memset(ones_b[:], 1.0).then_inc(s["onesb_done"], 1)
            pool.wait_ge(s["onesb_done"], 1)
            g.affine_select(out=tri_b[:], in_=ones_b[:], compare_op=ALU.is_gt, fill=0.0, base=0,
                            pattern=[[1, 128]], channel_multiplier=-1).then_inc(s["tri_done"], 1)
            g.iota(iota_e[:], pattern=[[1, E]], base=0, channel_multiplier=0,
                   allow_small_or_imprecise_dtypes=True).then_inc(s["iota_done"], 1)
            pool.wait_ge(s["half_done"], 1)
            pool.wait_ge(s["ve_done"], 1)
            for i in range(2):
                g.tensor_tensor(rstd[0][:, 2 * i:2 * i + 2], var_eps[0][:, 2 * i:2 * i + 2], half[:, 0:2], ALU.pow).then_inc(s["rstd_done"], 1)
            pool.wait_ge(s["route_in"], 32)
            g.tensor_copy(idx_f[:], idx_sb[:]).then_inc(s["idx_done"], 1)
            g.memset(mask[:], 0.0).then_inc(s["mask_z"], 1)
            pool.wait_ge(s["mask_z"], 1)
            g.affine_select(out=mask[:], in_=mask[:], compare_op=ALU.is_ge, fill=BIG, base=0,
                            pattern=[[0, XH], [-1, B]], channel_multiplier=1).then_inc(s["mask_done"], 1)
            g.iota(slot_no[:], pattern=[[1, CAP], [0, E]], base=0, channel_multiplier=0,
                   allow_small_or_imprecise_dtypes=True).then_inc(s["slot_done"], 1)
            pool.wait_ge(s["x_in"], 16)
            pool.wait_ge(s["rows_in"], 16)
            g.tensor_tensor(xbp[:], x_sb[:], row_sb[:, 0, :].rearrange("p (o d) -> p o d", o=1).to_broadcast([128, S, D]),
                            ALU.add).then_inc(s["xbp_done"], 1)
            g.memset(tor[:], 0.0).then_inc(s["tor_z"], 1)
            pool.wait_ge(s["tor_z"], 1)
            for i in range(S):
                for j in range(S):
                    n = (i == j) + ((i + 1) % S == j) + ((i - 1) % S == j)
                    if n:
                        g.memset(tor[:, i, j:j + 1], float(n)).then_inc(s["tor_done"], 1)
            pool.wait_ge(s["pick_done"], TOPK)
            for j in range(TOPK):
                g.tensor_tensor(pick_w[:, j], pick[:, j], wt_sb[:, :, j:j + 1].to_broadcast([128, S, E]), ALU.mult).then_inc(s["pickw_done"], 1)
            pool.wait_ge(s["pickw_done"], TOPK)
            g.tensor_tensor(gate[:], pick_w[:, 0], pick_w[:, 1], ALU.add).then_inc(s["gate_done"], 1)
            pool.wait_ge(s["gate_done"], 1)
            g.tensor_copy(gate3[:, :, 0], gate[:]).then_inc(s["gatehi_done"], 1)
            pool.wait_ge(s["gatehi_done"], 1)
            g.tensor_tensor(gate_r[:, 0], gate[:], gate3[:, :, 0], ALU.subtract).then_inc(s["gater_done"], 1)
            pool.wait_ge(s["gater_done"], 1)
            g.tensor_copy(gate3[:, :, 1], gate_r[:, 0]).then_inc(s["gatemid_done"], 1)
            pool.wait_ge(s["gatemid_done"], 1)
            g.tensor_tensor(gate_r[:, 1], gate_r[:, 0], gate3[:, :, 1], ALU.subtract).then_inc(s["gater2_done"], 1)
            pool.wait_ge(s["gater2_done"], 1)
            g.tensor_copy(gate3[:, :, 2], gate_r[:, 1]).then_inc(s["gate3_done"], 1)
            for t in range(S):
                pool.wait_ge(s["ve_done"], 2 + t)
                g.tensor_tensor(rstd[1][:, t:t + 1], var_eps[1][:, t:t + 1], half[:, 0:1], ALU.pow).then_inc(s["rstd_done"], 1)
            for t in range(1, S):
                pool.wait_ge(s["qkv_done"], t + 1)
                g.tensor_tensor(qk[:, 0:t, t], qkv[:, 0:t, 0], qkv[:, t:t + 1, 1].to_broadcast([128, t, D]), ALU.mult).then_inc(s["qk_pool"], 1)
            g.tensor_tensor(x1b[:], x1[:], row_sb[:, 1, :].rearrange("p (o d) -> p o d", o=1).to_broadcast([128, S, D]),
                            ALU.add).then_inc(s["x1b_done"], 1)
            t = S - 1
            pool.wait_ge(s["pn_done"], 2)
            g.tensor_tensor(pv[:, t].rearrange("p k (h d) -> p k h d", d=HD),
                            pn[:, t].rearrange("p k (h o) -> p k h o", o=1).to_broadcast([128, S, H, HD]),
                            qkv[:, :, 2].rearrange("p k (h d) -> p k h d", d=HD), ALU.mult).then_inc(s["pv_pool"], 1)
            for t in range(S):
                pool.wait_ge(s["ve_done"], 2 + S + t)
                g.tensor_tensor(rstd[2][:, t:t + 1], var_eps[2][:, t:t + 1], half[:, 0:1], ALU.pow).then_inc(s["rstd_done"], 1)
            g.tensor_tensor(x2b[:], x2[:], row_sb[:, 2, :].rearrange("p (o d) -> p o d", o=1).to_broadcast([128, S, D]),
                            ALU.add).then_inc(s["x2b_done"], 1)

        @block.scalar
        def _(act):
            a = nc.scalar
            act.dma_start(wc_sb[:], w_cross).then_inc(s["wc_in"], 16)
            a.preload_act_table(ACT.Exp)
            for h in range(XH):
                act.wait_ge(s["fold_ps"], h + 1)
                for n in range(2):
                    a.activation(fold_sb[:, n, h], bank[FOLD_BANK[h]][:, n * D:(n + 1) * D], ACT.Copy).then_inc(s["fold_done"], 1)
            for h in range(XH):
                act.wait_ge(s["kq_ps"], h + 1)
                a.activation(kq_sb[:, :, h, :], bank[KQ_BANK[h]][:].rearrange("p (s k) -> p s k", s=S), ACT.Copy,
                             scale=-float(DK) ** -0.5).then_inc(s["kq_done"], 1)
            act.wait_ge(s["vp_ps"], 1)
            a.activation(vp_sb[:, 0:2].rearrange("p s h d -> p (s h d)"), bank[VP_BANK[0]][:], ACT.Copy).then_inc(s["vp_done"], 1)
            def exponential(t, h):
                act.wait_ge(s["score_done"], XH * t + h + 1)
                a.activation(prob[:, t, h], nscore[:, t, h], ACT.Exp, bias=nmax[:, t, h:h + 1], scale=-1.0,
                             accum_out=psum_row[:, t, h:h + 1]).then_inc(s["exp_done"], 1)

            def probs_by_key(t):
                act.wait_ge(s["probT_ps"], t + 1)
                a.activation(probT[:, t].rearrange("p h k -> p (h k)"), bank[PROBT_BANK[t]][:, 0:XH * B],
                             ACT.Copy).then_inc(s["probT_done"], 1)

            for t in range(S):
                exponential(t, 0)
                if t:
                    probs_by_key(t - 1)
                exponential(t, 1)
            probs_by_key(S - 1)
            act.wait_ge(s["wqkv_ps"], 1)
            a.activation(wqkv_sb[:].rearrange("p a d -> p (a d)"), bank[WQKV_BANK][:, 0:3 * D], ACT.Copy).then_inc(s["wqkv_done"], 1)
            act.wait_ge(s["bqkv_ps"], 1)
            a.activation(bqkv[0:1, :], bank[BQKV_BANK][0:1, 0:3 * D], ACT.Copy).then_inc(s["bqkv_done"], 1)
            def turned(k):
                act.wait_ge(s["turn_ps"], k + 1)
                a.activation(takeT[:, k], bank[TURN_BANK[k % 2]][:], ACT.Copy).then_inc(s["turn_done"], 1)

            for t in range(S + 1):
                if t < S:
                    act.wait_ge(s["xnT_ps"], 1 + t + 1)
                    a.activation(xnT[1][:, t], bank[XNT1_BANK[t]][:, 0:B], ACT.Copy).then_inc(s["xnT_done"], 1)
                if t:
                    act.wait_ge(s["qkv_ps"], t)
                    a.activation(qkv[:, t - 1].rearrange("p a d -> p (a d)"), bank[QKV_BANK[t - 1]][:, 0:3 * D], ACT.Copy)\
                        .then_inc(s["qkv_done"], 1)
            for k in range(TURNS):
                turned(k)
            for i in range(2):
                act.wait_ge(s["scd_done"], i + 1)
                a.activation(expd[:, 2 * i:2 * i + 2].rearrange("p q k h -> p (q k h)"),
                             scd[:, 2 * i:2 * i + 2].rearrange("p q k h -> p (q k h)"), ACT.Exp).then_inc(s["expd_done"], 1)
            for k in range(TURNS, SC):
                turned(k)
            for t in range(S):
                act.wait_ge(s["oT_ps"], t + 1)
                a.activation(oT[:, t], bank[OT_BANK[t]][:, 0:B], ACT.Copy).then_inc(s["oT_done"], 1)
            for t in range(S):
                act.wait_ge(s["xn_done"], 2 * S + t + 1)
                a.activation(xn3[:, t, 0], xn[2][:, t], ACT.Copy).then_inc(s["split_hi"], 1)
                act.wait_ge(s["split_r"], t + 1)
                a.activation(xn3[:, t, 1], xn3_r[:, t], ACT.Copy).then_inc(s["split_mid"], 1)
            a.preload_act_table(ACT.Gelu)
            act.wait_ge(s["most_done"], 1)
            fullest = act.alloc_register("fullest_for_act")
            act.reg_load(fullest, most[0:1, 0:1])
            with act.If_lt(fullest, LIMIT + 1):
                def gelu(e):
                    if e >= 2:
                        act.wait_ge(s["yT_ps"], e - 1)
                    for c in range(2):
                        act.wait_ge(s["hr_ps"], 2 * e + c + 1)
                        a.activation(hidr[:, e % 2, 2 * c:2 * c + 2], bank[HR_BANK[c]][:, 0:2 * CAP].rearrange("p (c n) -> p c n", c=2),
                                     ACT.Gelu).then_inc(s["hr_done"], 1)

                def part_hi(k):
                    if k >= 2:
                        act.wait_ge(s["scatter_done"], k - 1)
                    act.wait_ge(s["ys_done"], k + 1)
                    a.activation(ys3[:, k % 2, 0], ys[:, k % 2], ACT.Copy).then_inc(s["yshi_done"], 1)

                def part_mid(k):
                    act.wait_ge(s["ysr_done"], k + 1)
                    a.activation(ys3[:, k % 2, 1], ysr[:, k % 2], ACT.Copy).then_inc(s["ysmid_done"], 1)

                act.wait_ge(s["xg_ps"], 2)
                a.activation(xg[:, 3 * CAP:6 * CAP], bank[GATHER_BANK[1]][:, 0:3 * CAP], ACT.Copy).then_inc(s["xg_act"], 1)
                for e in range(E):
                    gelu(e)
                    if e >= 2:
                        part_hi(e - 2)
                        part_mid(e - 2)
                part_hi(SC - 3)
                part_mid(SC - 3)
                for step in (part_hi, part_mid):
                    step(SC - 2)
                    step(SC - 1)
            with act.Else():
                for t in range(S):
                    act.wait_ge(s["xnT_ps"], 1 + S + t + 1)
                    a.activation(xnT[2][:, t], bank[XNT2_BANK[t]][:, 0:B], ACT.Copy).then_inc(s["xnT_done"], 1)
                for e in range(E):
                    if e >= 2:
                        act.wait_ge(s["y_ps"], S * (e - 1))
                    for c in range(FC):
                        act.wait_ge(s["h_ps"], FC * e + c + 1)
                        a.activation(hid[:, e % 2, c], bank[H_BANK[c]][:], ACT.Gelu).then_inc(s["h_done"], 1)

        @block.vector
        def _(dve):
            v = nc.vector

            def normalise(n, t, done_stats, done_mv, ve):
                dve.wait_ge(s["stats_done"], done_stats)
                v.bn_aggr(mv[n][:, t], stats[n][:, t]).then_inc(s["mv_done"], 1)

            v.memset(warm[:], 0.0).then_inc(s["warm_done"], 1)
            v.memset(picked[:], 0.0).then_inc(s["picked_z"], 1)
            dve.wait_ge(s["ident_done"], 1)
            v.tensor_reduce(owner[:], ident[:].rearrange("p (n e) -> p e n", e=E), AX.X, ALU.add).then_inc(s["owner_done"], 1)
            dve.wait_ge(s["x_in"], 16)
            for t in range(S):
                v.bn_stats(stats[0][:, t], x_sb[:, t]).then_inc(s["stats_done"], 1)
            for t in range(S):
                normalise(0, t, t + 1, None, None)
            dve.wait_ge(s["mv_done"], S)
            v.tensor_scalar(var_eps[0][:], mv[0][:, :, 1], EPS, None, ALU.add).then_inc(s["ve_done"], 1)
            for t in range(S):
                dve.wait_ge(s["rstd_done"], t // 2 + 1)
                v.tensor_scalar(xn[0][:, t], x_sb[:, t], mv[0][:, t, 0:1], rstd[0][:, t:t + 1], ALU.subtract,
                                ALU.mult).then_inc(s["xn_done"], 1)
            dve.wait_ge(s["idx_done"], 1)
            dve.wait_ge(s["iota_done"], 1)
            for j in range(TOPK):
                v.tensor_tensor(pick[:, j], idx_f[:, :, j:j + 1].to_broadcast([128, S, E]),
                                iota_e[:].rearrange("p (o e) -> p o e", o=1).to_broadcast([128, S, E]),
                                ALU.is_equal).then_inc(s["pick_done"], 1)
            dve.wait_ge(s["pick_done"], TOPK)
            dve.wait_ge(s["picked_z"], 1)
            v.tensor_tensor(picked[:, 0:S], pick[:, 0], pick[:, 1], ALU.max).then_inc(s["picked_done"], 1)
            dve.wait_ge(s["xnT_ps"], 1)
            for i in range(2):
                v.tensor_copy(xnT[0][:, 2 * i:2 * i + 2].rearrange("p s b -> p (s b)"), bank[XNT_BANK][:, 2 * i * B:(2 * i + 2) * B])\
                    .then_inc(s["xnT0_done"], 1)
            dve.wait_ge(s["rank_ps"], 1)
            v.scalar_tensor_tensor(out=code0[:], in0=picked[:, 0:S], scalar=-CODE,
                                   in1=bank[RANK_BANK][:, 0:S * E].rearrange("p (t e) -> p t e", e=E),
                                   op0=ALU.mult, op1=ALU.add).then_inc(s["code_done"], 1)
            v.tensor_reduce(most[:], bank[RANK_BANK][:, S * E:(S + 1) * E], AX.X, ALU.max).then_inc(s["most_done"], 1)
            dve.wait_ge(s["code_done"], 1)
            v.tensor_scalar(code[:], code0[:], CODE, None, ALU.add).then_inc(s["code_done"], 1)

            dve.wait_ge(s["mask_done"], 1)
            for t in range(S):
                dve.wait_ge(s["score_ps"], t + 1)
                for h in range(XH):
                    v.tensor_tensor_reduce(out=nscore[:, t, h], in0=bank[SCORE_BANK[t]][:, h * B:(h + 1) * B], in1=mask[:, h],
                                           scale=1.0, scalar=3.0e38, op0=ALU.add, op1=ALU.min,
                                           accum_out=nmax[:, t, h:h + 1]).then_inc(s["score_done"], 1)
            def slots_taken(t):
                dve.wait_ge(s["slot_done"], 1)
                dve.wait_ge(s["code_done"], 2)
                v.tensor_tensor(take[:, t], slot_no[:], code[:, t:t + 1].to_broadcast([128, CAP, E]),
                                ALU.is_equal).then_inc(s["take_done"], 1)

            slots_taken(0)
            dve.wait_ge(s["vp_ps"], 2)
            v.tensor_copy(vp_sb[:, 2:4].rearrange("p s h d -> p (s h d)"), bank[VP_BANK[1]][:]).then_inc(s["vp_done1"], 1)
            def row_sums(t):
                dve.wait_ge(s["exp_done"], XH * (t + 1))
                v.reciprocal(rsum[:, t], psum_row[:, t]).then_inc(s["rsum_done"], 1)

            def residual_a(t):
                dve.wait_ge(s["rsum_done"], t + 1)
                dve.wait_ge(s["xo_ps"], t + 1)
                v.scalar_tensor_tensor(out=x1a[:, t], in0=bank[XO_BANK[t]][:, 0:D], scalar=rsum[:, t, 0:1], in1=xbp[:, t],
                                       op0=ALU.mult, op1=ALU.add).then_inc(s["x1a_done"], 1)

            def residual_b(t):
                dve.wait_ge(s["x1a_done"], t + 1)
                v.scalar_tensor_tensor(out=x1[:, t], in0=bank[XO_BANK[t]][:, D:2 * D], scalar=rsum[:, t, 1:2],
                                       in1=x1a[:, t], op0=ALU.mult, op1=ALU.add).then_inc(s["x1_done"], 1)

            def norm_stats(n, src, ready, t):
                dve.wait_ge(s[ready], t + 1)
                v.bn_stats(stats[n][:, t], src[:, t]).then_inc(s["stats_done"], 1)

            def norm_mv(n, t):
                dve.wait_ge(s["stats_done"], n * S + t + 1)
                v.bn_aggr(mv[n][:, t], stats[n][:, t]).then_inc(s["mv_done"], 1)

            def norm_eps(n, t):
                dve.wait_ge(s["mv_done"], n * S + t + 1)
                v.tensor_scalar(var_eps[n][:, t:t + 1], mv[n][:, t, 1:2], EPS, None, ALU.add).then_inc(s["ve_done"], 1)

            def norm_apply(n, src, t):
                dve.wait_ge(s["rstd_done"], 2 + (n - 1) * S + t + 1)
                v.tensor_scalar(xn[n][:, t], src[:, t], mv[n][:, t, 0:1], rstd[n][:, t:t + 1], ALU.subtract,
                                ALU.mult).then_inc(s["xn_done"], 1)

            def products(t):
                dve.wait_ge(s["qkv_done"], t + 1)
                v.tensor_tensor(qk[:, t, 0:t + 1], qkv[:, t:t + 1, 0].to_broadcast([128, t + 1, D]), qkv[:, 0:t + 1, 1],
                                ALU.mult).then_inc(s["qk_done"], 1)

            def head_sums(t):
                dve.wait_ge(s["qk_done"], t + 1)
                v.tensor_reduce(sc0[:, t, 0:t + 1], qk[:, t, 0:t + 1].rearrange("p k (h d) -> p k h d", d=HD), AX.X,
                                ALU.add).then_inc(s["sc0_done"], 1)
                if t:
                    dve.wait_ge(s["qk_pool"], t)
                    v.tensor_reduce(sc0[:, 0:t, t], qk[:, 0:t, t].rearrange("p q (h d) -> p q h d", d=HD), AX.X,
                                    ALU.add).then_inc(s["sc0_done"], 1)

            dve.wait_ge(s["rows_in"], 16)
            dve.wait_ge(s["xbp_done"], 1)
            for w in range(S + 1):
                if w < S:
                    row_sums(w)
                if w:
                    norm_mv(1, w - 1)
                if w < S:
                    residual_a(w)
                if w:
                    norm_eps(1, w - 1)
                if w < S:
                    residual_b(w)
                    norm_stats(1, x1, "x1_done", w)
                if w:
                    norm_apply(1, x1, w - 1)
            for t in range(S):
                if t:
                    slots_taken(t)
                products(t)
                if t:
                    head_sums(t - 1)
            head_sums(S - 1)

            def wide(ap):
                return ap.rearrange("p q (o h) -> p q o h", o=1).to_broadcast([128, 2, S, H])

            def halves(step):
                for i in range(2):
                    step(i, slice(2 * i, 2 * i + 2))

            def add_toroidal(i, q):
                dve.wait_ge(s["tor_done"], 3 * S)
                dve.wait_ge(s["sc0_done"], 2 * S - 1)
                v.scalar_tensor_tensor(out=sc[:, q].rearrange("p q k h -> p (q k) h"), in0=sc0[:, q].rearrange("p q k h -> p (q k) h"),
                                       scalar=QSCALE, in1=tor[:, q].rearrange("p q (k o) -> p (q k) o", o=1).to_broadcast([128, 2 * S, H]),
                                       op0=ALU.mult, op1=ALU.add).then_inc(s["sc_done"], 1)

            def row_max(i, q):
                dve.wait_ge(s["sc_done"], i + 1)
                v.tensor_reduce(scm[:, q], sc[:, q].rearrange("p q k h -> p q h k"), AX.X, ALU.max).then_inc(s["scm_done"], 1)

            def less_max(i, q):
                dve.wait_ge(s["scm_done"], i + 1)
                v.tensor_tensor(scd[:, q], sc[:, q], wide(scm[:, q]), ALU.subtract).then_inc(s["scd_done"], 1)

            def exp_sum(i, q):
                dve.wait_ge(s["expd_done"], i + 1)
                v.tensor_reduce(exps[:, q], expd[:, q].rearrange("p q k h -> p q h k"), AX.X, ALU.add).then_inc(s["exps_done"], 1)

            def inverse(i, q):
                dve.wait_ge(s["exps_done"], i + 1)
                v.reciprocal(expr[:, q], exps[:, q]).then_inc(s["expr_done"], 1)

            def probabilities(i, q):
                dve.wait_ge(s["expr_done"], i + 1)
                v.tensor_tensor(pn[:, q], expd[:, q], wide(expr[:, q]), ALU.mult).then_inc(s["pn_done"], 1)

            for step in (add_toroidal, row_max, less_max):
                halves(step)
            for step in (exp_sum, inverse, probabilities):
                halves(step)

            def weigh_values(q):
                dve.wait_ge(s["pn_done"], q // 2 + 1)
                v.tensor_tensor(pv[:, q].rearrange("p k (h d) -> p k h d", d=HD),
                                pn[:, q].rearrange("p k (h o) -> p k h o", o=1).to_broadcast([128, S, H, HD]),
                                qkv[:, :, 2].rearrange("p k (h d) -> p k h d", d=HD), ALU.mult).then_inc(s["pv_done"], 1)

            def add_pairs(q):
                if q == S - 1:
                    dve.wait_ge(s["pv_pool"], 1)
                else:
                    dve.wait_ge(s["pv_done"], q + 1)
                v.tensor_tensor(pv2[:, q], pv[:, q, 0:2], pv[:, q, 2:4], ALU.add).then_inc(s["pv2_done"], 1)

            for q in range(S - 1):
                weigh_values(q)
            for q in range(UNPAIRED, S):
                add_pairs(q)
            dve.wait_ge(s["x1b_done"], 1)

            def residual_2(t):
                dve.wait_ge(s["so_ps"], t + 1)
                v.tensor_tensor(x2[:, t], bank[SO_BANK[t]][:, 0:D], x1b[:, t], ALU.add).then_inc(s["x2_done"], 1)

            def split_rest(t):
                dve.wait_ge(s["split_hi"], t + 1)
                v.tensor_tensor(xn3_r[:, t], xn[2][:, t], xn3[:, t, 0], ALU.subtract).then_inc(s["split_r"], 1)

            def split_low(t):
                dve.wait_ge(s["split_mid"], t + 1)
                v.tensor_tensor(xn3[:, t, 2], xn3_r[:, t], xn3[:, t, 1], ALU.subtract).then_inc(s["split_lo"], 1)

            for w in range(S + 3):
                if 0 < w <= S:
                    norm_mv(2, w - 1)
                if w < S:
                    residual_2(w)
                if 0 < w <= S:
                    norm_eps(2, w - 1)
                if 1 < w <= S + 1:
                    split_rest(w - 2)
                if w > 2:
                    split_low(w - 3)
                if w < S:
                    norm_stats(2, x2, "x2_done", w)
                if 0 < w <= S:
                    norm_apply(2, x2, w - 1)
            dve.wait_ge(s["owner_done"], 1)
            dve.wait_ge(s["sgate_ps"], 1)
            v.tensor_tensor(shared[:], bank[GATE_BANK][:, 3 * E:6 * E].rearrange("p (g e) -> p g e", g=3),
                            owner[:].rearrange("p (o e) -> p o e", o=1).to_broadcast([128, 3, E]), ALU.mult)\
                .then_inc(s["sgates_done"], 1)
            v.tensor_reduce(slot_gate[:, 0:E], bank[GATE_BANK][:, 0:3 * E].rearrange("p (k g) -> p k g", g=3), AX.X, ALU.add)\
                .then_inc(s["sgates_done"], 1)
            dve.wait_ge(s["sgates_done"], 2)
            v.tensor_reduce(slot_gate[:, E:SC], shared[:], AX.XY, ALU.add).then_inc(s["sgate_done"], 1)
            dve.wait_ge(s["most_done"], 1)
            fullest = dve.alloc_register("fullest_for_dve")
            dve.reg_load(fullest, most[0:1, 0:1])
            with dve.If_lt(fullest, LIMIT + 1):
                for n in (0, 2):
                    lo, hi = 3 * n * CAP, min(3 * (n + 1) * CAP, SLOTS)
                    dve.wait_ge(s["xg_ps"], n + 1)
                    v.tensor_copy(xg[:, lo:hi], bank[GATHER_BANK[n]][:, 0:hi - lo]).then_inc(s["xg_done"], 1)
                dve.wait_ge(s["sgate_done"], 1)

                def by_feature(e):
                    dve.wait_ge(s["yT_ps"], e + 1)
                    v.tensor_copy(yT[:, :, e], bank[YT_BANK][:, 0:CAP]).then_inc(s["yT_done"], 1)

                def gated(k):
                    dve.wait_ge(s["ys_ps"], k + 1)
                    v.tensor_scalar(ys[:, k % 2], bank[YS_BANK[k]][:, 0:D], slot_gate[:, k:k + 1], None, ALU.mult).then_inc(s["ys_done"], 1)

                def gated_rest(k):
                    dve.wait_ge(s["yshi_done"], k + 1)
                    v.tensor_tensor(ysr[:, k % 2], ys[:, k % 2], ys3[:, k % 2, 0], ALU.subtract).then_inc(s["ysr_done"], 1)

                def gated_low(k):
                    dve.wait_ge(s["ysmid_done"], k + 1)
                    v.tensor_tensor(ys3[:, k % 2, 2], ysr[:, k % 2], ys3[:, k % 2, 1], ALU.subtract).then_inc(s["yslo_done"], 1)

                for e in range(E):
                    by_feature(e)
                    if e:
                        for step in (gated, gated_rest, gated_low):
                            step(e - 1)
                for step in (gated, gated_rest, gated_low):
                    step(SC - 2)
                    step(SC - 1)
                dve.wait_ge(s["x2b_done"], 1)
                for t in range(S):
                    dve.wait_ge(s["sum_ps"], t + 1)
                    v.tensor_tensor(res[:, t], bank[SUM_BANK[t]][:, 0:D], x2b[:, t], ALU.add).then_inc(s["res_done"], 1)
            with dve.Else():
                dve.wait_ge(s["gate_done"], 1)
                dve.wait_ge(s["x2b_done"], 1)
                for e in range(E):
                    for t in range(S):
                        dve.wait_ge(s["y_ps"], S * e + t + 1)
                        if e:
                            dve.wait_ge(s["acc_done"], S * (e - 1) + t + 1)
                        v.scalar_tensor_tensor(out=acc[:, e % 2, t], in0=bank[Y_BANK[t]][:, 0:D],
                                               scalar=gate[:, t, e:e + 1], in1=acc[:, (e - 1) % 2, t] if e else x2b[:, t],
                                               op0=ALU.mult, op1=ALU.add).then_inc(s["acc_done"], 1)

        @block.tensor
        def _(pe):
            mm, tr = nc.tensor.matmul, nc.tensor.transpose
            zero = nc.const_aps.tensor(0.0, [128, 512], F32)

            def keep_warm(n, cols=512, where=WARM_BANK):
                for _ in range(n):
                    mm(bank[where][:, 0:cols], warm[:, 0:128], warm[:, 0:cols], start=True, stop=True)

            for n in W0:
                mm(bank[WARM_BANK][0:32, 0:n], zero[:, 0:32], zero[:, 0:n], start=True, stop=True)
            pe.wait_ge(s["warm_done"], 1)
            keep_warm(W1)
            pe.wait_ge(s["wc_in"], 16)
            for h in range(XH):
                r = slice(h * DK, (h + 1) * DK)
                for n in range(2):
                    last = mm(bank[FOLD_BANK[h]][:, n * D:(n + 1) * D], wc_sb[r, 1 + n, :], wc_sb[r, 3 * n, :], start=True, stop=True)
                last.then_inc(s["fold_ps"], 1)

            def keys(h):
                pe.wait_ge(s["fold_done"], 2 * h + 1)
                mm(bank[KQ_BANK[h]][:], fold_sb[:, 0, h], ctx_sb[:].rearrange("p s k -> p (s k)"), start=True, stop=True).then_inc(s["kq_ps"], 1)

            def values(p):
                for t in (2 * p, 2 * p + 1):
                    last = mm(bank[VP_BANK[p]][:, t % 2 * 256:t % 2 * 256 + 256], ctx_sb[:, t], fold_sb[:, 1].rearrange("p h d -> p (h d)"),
                              start=True, stop=True)
                last.then_inc(s["vp_ps"], 1)

            pe.wait_ge(s["ctx_in"], 16)
            keys(0)
            keys(1)
            pe.wait_ge(s["ident_done"], 1)
            for t in range(S):
                pe.wait_ge(s["xn_done"], t + 1)
                last = tr(bank[XNT_BANK][:, t * B:(t + 1) * B], xn[0][:, t], ident[:])
            last.then_inc(s["xnT_ps"], 1)
            pe.wait_ge(s["fold_done"], 2 * XH)
            pe.wait_ge(s["picked_done"], 1)
            pe.wait_ge(s["tri_done"], 1)
            mm(bank[RANK_BANK][:, 0:(S + 1) * E], tri_b[:], picked[:].rearrange("p t e -> p (t e)"), start=True, stop=False)
            for t in range(S):
                last = mm(bank[RANK_BANK][:, (t + 1) * E:(S + 1) * E], ones_b[:],
                          picked[:, t:t + 1].to_broadcast([128, S - t, E]), start=False, stop=(t == S - 1))
            last.then_inc(s["rank_ps"], 1)
            values(0)
            pe.wait_ge(s["kq_done"], 2)
            for t in range(S):
                pe.wait_ge(s["xnT0_done"], 1 if t == 0 else 2)
                mm(bank[SCORE_BANK[t]][:, 0:XH * B], xnT[0][:, t], kq_sb[:, t].rearrange("p h k -> p (h k)"),
                   start=True, stop=True).then_inc(s["score_ps"], 1)

            def probs_turned(t):
                pe.wait_ge(s["score_done"], XH * (t + 1))
                for h in range(XH):
                    pe.wait_ge(s["exp_done"], XH * t + h + 1)
                    last = tr(bank[PROBT_BANK[t]][:, h * B:(h + 1) * B], prob[:, t, h], ident[:])
                last.then_inc(s["probT_ps"], 1)

            def probs_out(t):
                pe.wait_ge(s["probT_done"], t + 1)
                pe.wait_ge(s["vp_done"], 1)
                if t:
                    pe.wait_ge(s["vp_done1"], 1)
                for h in range(XH):
                    last = mm(bank[XO_BANK[t]][:, h * D:(h + 1) * D], probT[:, t, h], vp_sb[:, t, h], start=True, stop=True)
                last.then_inc(s["xo_ps"], 1)

            probs_turned(0)
            values(1)
            probs_out(0)
            probs_turned(1)
            pe.wait_ge(s["ws_in"], 16)
            mm(bank[WQKV_BANK][:, 0:3 * D], ws_sb[:, 0], ws_sb[:, 1:4].rearrange("p a d -> p (a d)"), start=True, stop=True).then_inc(s["wqkv_ps"], 1)
            probs_out(1)
            probs_turned(2)
            pe.wait_ge(s["bias_in"], 32)
            pe.wait_ge(s["most_done"], 1)
            mm(bank[BQKV_BANK][0:1, 0:3 * D], btor_sb[:], ws_sb[:, 1:4].rearrange("p a d -> p (a d)"), start=True, stop=True)\
                .then_inc(s["bqkv_ps"], 1)
            probs_out(2)
            probs_turned(3)
            probs_out(3)

            def transpose_1(t):
                pe.wait_ge(s["xn_done"], S + t + 1)
                tr(bank[XNT1_BANK[t]][:, 0:B], xn[1][:, t], ident[:]).then_inc(s["xnT_ps"], 1)

            def bias_1(t):
                if t == 0:
                    pe.wait_ge(s["ones_done"], 1)
                    pe.wait_ge(s["bqkv_done"], 1)
                elif t == 2:
                    pe.wait_ge(s["xnT_done"], 1)
                elif t == 3:
                    pe.wait_ge(s["x1_done"], XO_BANK.index(QKV_BANK[3]) + 1)
                mm(bank[QKV_BANK[t]][:, 0:3 * D], ones[:], bqkv[:], start=True, stop=False)

            def project(t):
                pe.wait_ge(s["xnT_done"], t + 1)
                mm(bank[QKV_BANK[t]][:, 0:3 * D], xnT[1][:, t], wqkv_sb[:].rearrange("p a d -> p (a d)"), start=False, stop=True)\
                    .then_inc(s["qkv_ps"], 1)

            def chunk(t, k):
                return take[:, t, 0:CHUNK, k] if k < E else take[:, t, CHUNK:CAP].rearrange("p n e -> p (n e)")

            def turn(k):
                if k > 1:
                    pe.wait_ge(s["turn_done"], k - 1)
                for t in range(S):
                    if k == 0:
                        pe.wait_ge(s["take_done"], t + 1)
                    last = mm(bank[TURN_BANK[k % 2]][:, t * B:(t + 1) * B], chunk(t, k), ident_b[:], start=True, stop=True)
                last.then_inc(s["turn_ps"], 1)

            for t in range(S):
                if t == 0:
                    bias_1(0)
                transpose_1(t)
                if t:
                    bias_1(t)
                project(t)
            pe.wait_ge(s["identb_done"], 1)
            pe.wait_ge(s["xnT_done"], S)
            pe.wait_ge(s["qkv_done"], S)
            for k in range(SC):
                turn(k)
                keep_warm(W3, 512, SO_BANK[0])
            keep_warm(W4, 512, SO_BANK[0])
            pe.wait_ge(s["qkv_done"], S)
            def summed(q):
                if q < UNPAIRED:
                    pe.wait_ge(s["pv_done"], q + 1)
                    terms = [pv[:, q, k] for k in range(S)]
                else:
                    pe.wait_ge(s["pv2_done"], q - UNPAIRED + 1)
                    terms = [pv2[:, q, k] for k in range(S // 2)]
                for k, term in enumerate(terms):
                    last = mm(bank[OT_BANK[q]][:, 0:B], term, ident[:], start=(k == 0), stop=(k == len(terms) - 1))
                last.then_inc(s["oT_ps"], 1)

            def through_out_w(q):
                pe.wait_ge(s["oT_done"], q + 1)
                mm(bank[SO_BANK[q]][:, 0:D], oT[:, q], ws_sb[:, 4], start=True, stop=True).then_inc(s["so_ps"], 1)

            for q in range(S):
                summed(q)
                if q:
                    through_out_w(q - 1)
            through_out_w(S - 1)
            def gather(t):
                for part in range(3):
                    pe.wait_ge(s[("split_hi", "split_mid", "split_lo")[part]], t + 1)
                    for n in range(3):
                        lo, hi = 3 * n, min(3 * (n + 1), E)
                        last = mm(bank[GATHER_BANK[n]][:, 0:(hi - lo) * CAP], xn3[:, t, part],
                                  take[:, t, :, lo:hi].rearrange("p n e -> p e n"),
                                  start=(t == 0 and part == 0), stop=(t == S - 1 and part == 2))
                        if t == S - 1 and part == 2:
                            last.then_inc(s["xg_ps"], 1)

            pe.wait_ge(s["turn_done"], SC)
            pe.wait_ge(s["x2_done"], SO_BANK.index(GATE_BANK) + 1)
            pe.wait_ge(s["gate3_done"], 1)
            for k in range(SC):
                for t in range(S):
                    cols, gates = ((slice(3 * k, 3 * k + 3), gate3[:, t, :, k]) if k < E else
                                   (slice(3 * E, 6 * E), gate3[:, t].rearrange("p g e -> p (g e)")))
                    last = mm(bank[GATE_BANK][:, cols], chunk(t, k), gates, start=(t == 0), stop=(t == S - 1))
            last.then_inc(s["sgate_ps"], 1)
            for t in range(S):
                gather(t)
            pe.wait_ge(s["most_done"], 1)
            fullest = pe.alloc_register("fullest_for_pe")
            pe.reg_load(fullest, most[0:1, 0:1])
            with pe.If_lt(fullest, LIMIT + 1):
                def hidden(e):
                    pe.wait_ge(w1_in[e // 2], 16)
                    if e == 0:
                        pe.wait_ge(s["x2_done"], S)
                        pe.wait_ge(s["sgates_done"], 2)
                    if 3 <= e < 6:
                        pe.wait_ge(s["xg_act"], 1)
                    else:
                        pe.wait_ge(s["xg_done"], 2 if e >= 6 else 1)
                    for c in range(FC):
                        if e and c % 2 == 0:
                            pe.wait_ge(s["hr_done"], 2 * (e - 1) + c // 2 + 1)
                        last = mm(bank[HR_BANK[c // 2]][:, c % 2 * CAP:(c % 2 + 1) * CAP], w1_sb[:, e, c * 128:(c + 1) * 128],
                                  xg[:, e * CAP:(e + 1) * CAP], start=True, stop=True)
                        if c % 2:
                            last.then_inc(s["hr_ps"], 1)

                def expert_out(e):
                    pe.wait_ge(w2_in[e // 2], 16)
                    pe.wait_ge(s["hr_done"], 2 * (e + 1))
                    if e:
                        pe.wait_ge(s["yT_done"], e)
                    for c in range(FC):
                        last = mm(bank[YT_BANK][:, 0:CAP], w2_sb[:, e, c], hidr[:, e % 2, c], start=(c == 0), stop=(c == FC - 1))
                    last.then_inc(s["yT_ps"], 1)

                def by_slot(k):
                    pe.wait_ge(s["yT_done"], last_expert(k) + 1)
                    if 0 < k < SC - 1:
                        pe.wait_ge(s["ys_done"], k)
                    y = yT[:, 0:CHUNK, k] if k < E else yT[:, CHUNK:CAP].rearrange("p n e -> p (n e)")
                    tr(bank[YS_BANK[k]][:, 0:D], y, ident[:]).then_inc(s["ys_ps"], 1)

                def scatter(k, part):
                    if k == 0 and part == 0:
                        pe.wait_ge(s["xg_done"], 2)
                        pe.wait_ge(s["xg_act"], 1)
                    pe.wait_ge(s[("yshi_done", "ysmid_done", "yslo_done")[part]], k + 1)
                    for t in range(S):
                        last = mm(bank[SUM_BANK[t]][:, 0:D], takeT[:, k, t * B:(t + 1) * B], ys3[:, k % 2, part],
                                  start=(k == 0 and part == 0), stop=(k == SC - 1 and part == 2))
                        if k == SC - 1 and part == 2:
                            last.then_inc(s["sum_ps"], 1)
                    if k < SC - 1 and part == 2:
                        last.then_inc(s["scatter_done"], 1)

                for e in range(E):
                    hidden(e)
                    if e:
                        expert_out(e - 1)
                    if e >= 2:
                        by_slot(e - 2)
                    if e >= 3:
                        for part in range(3):
                            scatter(e - 3, part)
                expert_out(E - 1)
                by_slot(SC - 3)
                for part in range(3):
                    scatter(SC - 4, part)
                by_slot(SC - 2)
                by_slot(SC - 1)
                for part in range(3):
                    scatter(SC - 3, part)
                for part in range(3):
                    scatter(SC - 2, part)
                    scatter(SC - 1, part)
            with pe.Else():
                pe.wait_ge(s["sgates_done"], 2)
                for t in range(S):
                    keep_warm(W5)
                    pe.wait_ge(s["xn_done"], 2 * S + t + 1)
                    tr(bank[XNT2_BANK[t]][:, 0:B], xn[2][:, t], ident[:]).then_inc(s["xnT_ps"], 1)
                pe.wait_ge(s["xnT_done"], 2 * S)
                pe.wait_ge(s["x2_done"], S)
                pe.wait_ge(s["sgates_done"], 2)

                def hidden(e):
                    pe.wait_ge(w1_in[e // 2], 16)
                    for c in range(FC):
                        if e:
                            pe.wait_ge(s["h_done"], FC * (e - 1) + c + 1)
                        mm(bank[H_BANK[c]][:], w1_sb[:, e, c * 128:(c + 1) * 128], xnT[2][:].rearrange("p s b -> p (s b)"),
                           start=True, stop=True).then_inc(s["h_ps"], 1)

                def expert_out(e):
                    pe.wait_ge(w2_in[e // 2], 16)
                    pe.wait_ge(s["h_done"], FC * (e + 1))
                    for t in range(S):
                        if e:
                            pe.wait_ge(s["acc_done"], S * (e - 1) + t + 1)
                        for c in range(FC):
                            last = mm(bank[Y_BANK[t]][:, 0:D], hid[:, e % 2, c, t * B:(t + 1) * B], w2_sb[:, e, c],
                                      start=(c == 0), stop=(c == FC - 1))
                        last.then_inc(s["y_ps"], 1)

                for e in range(E):
                    hidden(e)
                    if e:
                        expert_out(e - 1)
                expert_out(E - 1)


_ORDER = ["x", "ctxT", "w_cross", "w_self", "cols", "in_bias", "rows", "exp_idx", "exp_wt", "w1", "w2"]


def kernel(x, ctx_1024, L0_xattn_Wq, L0_xattn_Wk, L0_xattn_Wv, L0_xattn_Wp, L0_xattn_bp, L0_attn_w_tor, L0_attn_b_tor,
           L0_attn_in_proj_w, L0_attn_in_proj_b, L0_attn_out_w, L0_attn_out_b, L0_ffn_scores, L0_ffn_expert_weights,
           L0_ffn_expert_indices, L0_ffn_w1, L0_ffn_w2, L0_ffn_bias):
    import numpy as np
    import concourse.bacc as bacc
    from concourse import mybir as _mybir
    from concourse.bass_utils import run_bass_kernel_spmd

    A = np.asarray
    c = np.ascontiguousarray
    S, B, D = A(x).shape
    E, _, FF = A(L0_ffn_w1).shape
    ipw = A(L0_attn_in_proj_w)
    arrays = {
        "x": c(A(x)),
        "ctxT": c(A(ctx_1024).transpose(2, 0, 1)),
        "w_cross": c(np.stack([A(L0_xattn_Wq), A(L0_xattn_Wk), A(L0_xattn_Wv), A(L0_xattn_Wp).T], axis=1)),
        "w_self": c(np.concatenate([A(L0_attn_w_tor), ipw.T, A(L0_attn_out_w).T], axis=1).reshape(D, 5, D)),
        "cols": c(A(L0_attn_b_tor).reshape(D, 1)),
        "in_bias": c(A(L0_attn_in_proj_b).reshape(1, 3 * D)),
        "rows": c(np.stack([A(L0_xattn_bp), A(L0_attn_out_b), A(L0_ffn_bias)])),
        "exp_idx": c(A(L0_ffn_expert_indices).reshape(S, B, -1).transpose(1, 0, 2)),
        "exp_wt": c(A(L0_ffn_expert_weights).reshape(S, B, -1).transpose(1, 0, 2)),
        "w1": c(A(L0_ffn_w1).transpose(1, 0, 2)),
        "w2": c(A(L0_ffn_w2).reshape(E, FF // 128, 128, D).transpose(2, 0, 1, 3)),
    }
    nc = bacc.Bacc("TRN2", target_bir_lowering=False, num_devices=1)
    args = [nc.dram_tensor(f"in_{n}", arrays[n].shape, _mybir.dt.from_np(arrays[n].dtype), kind="ExternalInput").ap()
            for n in _ORDER]
    out = nc.dram_tensor("out_0", (S, B, D), _mybir.dt.float32, kind="ExternalOutput").ap()
    perceiver_layer(nc, *args, out)
    r = run_bass_kernel_spmd(nc, [{f"in_{n}": arrays[n] for n in _ORDER}], core_ids=[0])
    return r.results[0]["out_0"]
```

```python
from contextlib import ExitStack

import concourse.bass as bass
from concourse import mybir

ALU = mybir.AluOpType
ACT = mybir.ActivationFunctionType
AX = mybir.AxisListType
F32 = mybir.dt.float32
I32 = mybir.dt.int32
BF16 = mybir.dt.bfloat16


def perceiver_layer(nc, x, ctxT, w_cross, w_self, cols, in_bias, rows, exp_idx, exp_wt, w1, w2, out):
    S, B, D = x.shape
    XH, DK = 2, D // 2
    H, HD = 16, D // 16
    E, FF = w1.shape[1:]
    FC = FF // 128
    TOPK = 2
    QSCALE = float(HD) ** -0.5
    CHUNK = 128
    CAP = CHUNK + CHUNK // E
    SLOTS = E * CAP
    LIMIT = CAP
    SC = SLOTS // CHUNK
    CODE = 4096.0
    BIG = 1.0e13
    EPS = 1e-5
    FOLD_BANK = [0, 3]
    KQ_BANK = [1, 2]
    XNT_BANK = 5
    WQKV_BANK = 7
    BQKV_BANK = 4
    VP_BANK = [0, 3, 3, 4]
    SCORE_BANK = [6, 5, 1, 2]
    PROBT_BANK = SCORE_BANK
    XO_BANK = [0, 3, 6, 5]
    XNT1_BANK = [1, 2, 0, 3]
    QKV_BANK = [4, 7, 1, 6]
    OT_BANK = [2, 3, 4, 5]
    SO_BANK = [6, 1, 2, 3]
    RANK_BANK = 7
    WARM_BANK = 6
    TURN_BANK = [0, 7]
    GATE_BANK = 1
    GATHER_BANK = [0, 4, 5]
    HR_BANK = [[3, 2] if e == 1 else [6, 1] for e in range(E)]
    YT_BANK = 7
    YS_BANK = [2] * (SC - 1) + [6]
    SUM_BANK = [0, 4, 5, 3]
    XNT2_BANK = [0, 3, 4, 6]
    H_BANK = [7, 5, 1, 2]
    Y_BANK = [0, 3, 4, 6]
    TURNS = 6
    FIRST_WARM = [512, 512, 64]
    LAST_WARM = 2

    def last_expert(k):
        return min(k, E - 1)

    with ExitStack() as ctx:
        def sb(name, shape, dt=F32):
            return ctx.enter_context(nc.sbuf_tensor(name, shape, dt))

        def sem(name):
            return ctx.enter_context(nc.semaphore(name))

        bank = [ctx.enter_context(nc.psum_tensor(f"bank{i}", [128, 512], F32)) for i in range(8)]

        x_sb = sb("x_sb", [128, S, D])
        ctx_sb = sb("ctx_sb", [128, S, B])
        wc_sb = sb("wc_sb", [128, 4, D])
        ws_sb = sb("ws_sb", [128, 5, D])
        btor_sb = sb("btor_sb", [128, 1])
        row_sb = sb("row_sb", [128, 3, D])
        idx_sb = sb("idx_sb", [128, S, TOPK], I32)
        wt_sb = sb("wt_sb", [128, S, TOPK])
        w1_sb = sb("w1_sb", [128, E, FF])
        w2_sb = sb("w2_sb", [128, E, FC, D])

        ident = sb("ident", [128, 128])
        mask = sb("mask", [128, XH, B])
        tor = sb("tor", [128, S, S])
        half = sb("half", [128, S])

        fold_sb = sb("fold_sb", [128, 2, XH, D])
        kq_sb = sb("kq_sb", [128, S, XH, B])
        vp_sb = sb("vp_sb", [128, S, XH, D])
        wqkv_sb = sb("wqkv_sb", [128, 3, D])
        bqkv = sb("bqkv", [128, 3 * D])
        ones = sb("ones", [128, 128])
        warm = sb("warm", [128, 512], BF16)
        gate = sb("gate", [128, S, E])
        iota_e = sb("iota_e", [128, E])
        idx_f = sb("idx_f", [128, S, TOPK])
        pick = sb("pick", [128, TOPK, S, E])
        pick_w = sb("pick_w", [128, TOPK, S, E])

        stats = [sb(f"stats{i}", [128, S, 6]) for i in range(3)]
        mv = [sb(f"mv{i}", [128, S, 2]) for i in range(3)]
        var_eps = [sb(f"var_eps{i}", [128, S]) for i in range(3)]
        rstd = [sb(f"rstd{i}", [128, S]) for i in range(3)]
        xn = [sb(f"xn{i}", [128, S, D]) for i in range(3)]
        xnT = [sb(f"xnT{i}", [128, S, B]) for i in range(3)]

        xbp = sb("xbp", [128, S, D])
        nscore = sb("nscore", [128, S, XH, B])
        nmax = sb("nmax", [128, S, XH])
        prob = sb("prob", [128, S, XH, B])
        psum_row = sb("psum_row", [128, S, XH])
        rsum = sb("rsum", [128, S, XH])
        probT = sb("probT", [128, S, XH, B])
        x1a = sb("x1a", [128, S, D])
        x1 = sb("x1", [128, S, D])
        x1b = sb("x1b", [128, S, D])

        qkv = sb("qkv", [128, S, 3, D])
        qk = sb("qk", [128, S, S, D])
        head4 = sb("head4", [128, S - 1, H, 4])
        head2 = sb("head2", [128, S - 1, H, 2])
        sc0 = sb("sc0", [128, S, S, H])
        sc = sb("sc", [128, S, S, H])
        scm = sb("scm", [128, S, H])
        scd = sb("scd", [128, S, S, H])
        expd = sb("expd", [128, S, S, H])
        exps = sb("exps", [128, S, H])
        expr = sb("expr", [128, S, H])
        pn = sb("pn", [128, S, S, H])
        pv = sb("pv", [128, S, S, D])
        pv2 = sb("pv2", [128, S, S // 2, D])
        oT = sb("oT", [128, S, B])
        x2 = sb("x2", [128, S, D])
        x2b = sb("x2b", [128, S, D])

        tri_b = sb("tri_b", [128, 128], BF16)
        ones_b = sb("ones_b", [128, 128], BF16)
        ident_b = sb("ident_b", [128, 128], BF16)
        picked = sb("picked", [128, S + 1, E], BF16)
        code0 = sb("code0", [128, S, E])
        code = sb("code", [128, S, E], BF16)
        most = sb("most", [128, 1], I32)
        slot_no = sb("slot_no", [128, CAP, E], BF16)
        take = sb("take", [128, S, CAP, E], BF16)
        takeT = sb("takeT", [128, SC, S * B], BF16)
        owner = sb("owner", [128, E])
        gate3 = sb("gate3", [128, S, 3, E], BF16)
        gate_r = sb("gate_r", [128, 2, S, E])
        shared = sb("shared", [128, 3, E])
        slot_gate = sb("slot_gate", [128, SC])
        xn3 = sb("xn3", [128, S, 3, D], BF16)
        xn3_r = sb("xn3_r", [128, S, D])
        xg = sb("xg", [128, SLOTS])
        yT = sb("yT", [128, CAP, E])
        ys = sb("ys", [128, 3, D])
        ysr = sb("ysr", [128, 3, D])
        ys3 = sb("ys3", [128, 3, 3, D], BF16)

        hid = sb("hid", [128, 2, FC, S * B])
        acc = sb("acc", [128, 2, S, D])
        hidr = hid[:, :, :, 0:CAP]
        res = acc[:, 0]

        names = """x_in ctx_in ws_in route_in bias_in bqkv_zeroed rows_in most_done res_done out_done acc_done
        ident_zeroed ident_done ones_done ident_b_done half_done ones_b_done tri_done iota_done var_eps_done
        rstd_done idx_done mask_zeroed mask_done slot_done xbp_done tor_zeroed tor_done pick_done pickw_done
        gate_done gate_hi gate_rest gate_mid gate_rest2 gate3_done qkv_done qk_pool head4_done head2_done sc0_pool
        x1b_done expr_done pn_pool pv_pool pv2_pool x2b_done wc_in fold_ps fold_done kq_ps kq_done vp_ps vp_done
        score_done exp_done probT_ps probT_done wqkv_ps wqkv_done bqkv_ps bqkv_done turn_ps turn_done xnT_ps xnT_done
        qkv_ps scd_done expd_done oT_ps oT_done xn_done xn3_hi xn3_rest xn3_mid yT_ps hr_ps hr_done scatter_done
        ys_done ys_hi ys_rest ys_mid xg_ps xg_act y_ps h_ps h_done warm_done picked_zeroed owner_done stats_done
        mv_done picked_done xnT0_done rank_ps code_done score_ps take_done vp_mid_done rsum_done xo_ps x1a_done
        x1_done qk_done sc0_done sc_done scm_done exps_done pn_done pv_done pv2_done gates_ps gates_read so_ps
        x2_done xn3_lo slot_gate_done xg_done yT_done ys_ps ys_lo sum_ps""".split()
        s = {n: sem(n) for n in names}
        w1_in = [sem(f"w1_in{e}") for e in range(E // 2)]
        w2_in = [sem(f"w2_in{e}") for e in range(E // 2)]

        block = ctx.enter_context(nc.Block())

        @block.sync
        def _(sp):
            sp.dma_start(x_sb[:], x.rearrange("s b d -> b s d")).then_inc(s["x_in"], 16)
            sp.dma_start(ctx_sb[:], ctxT[:, :, 0:B]).then_inc(s["ctx_in"], 16)
            sp.dma_start(ws_sb[:], w_self).then_inc(s["ws_in"], 16)
            sp.dma_start(idx_sb[:], exp_idx).then_inc(s["route_in"], 16)
            sp.dma_start(wt_sb[:], exp_wt).then_inc(s["route_in"], 16)
            sp.dma_start(btor_sb[:], cols).then_inc(s["bias_in"], 16)
            sp.wait_ge(s["bqkv_zeroed"], 1)
            sp.dma_start(bqkv[32:33, :], in_bias).then_inc(s["bias_in"], 16)
            sp.dma_start(row_sb[:], rows.rearrange("(o r) d -> o r d", o=1).to_broadcast([128, 3, D])).then_inc(s["rows_in"], 16)
            for p in range(E // 2):
                sp.dma_start(w1_sb[:, 2 * p:2 * p + 2], w1[:, 2 * p:2 * p + 2]).then_inc(w1_in[p], 16)
                sp.dma_start(w2_sb[:, 2 * p:2 * p + 2], w2[:, 2 * p:2 * p + 2]).then_inc(w2_in[p], 16)
            sp.wait_ge(s["most_done"], 1)
            fullest = sp.alloc_register("fullest_for_sp")
            sp.reg_load(fullest, most[0:1, 0:1])
            with sp.If_lt(fullest, LIMIT + 1):
                for t in (0, 2):
                    sp.wait_ge(s["res_done"], t + 2)
                    sp.dma_start(out[t:t + 2].rearrange("s b d -> b s d"), res[:, t:t + 2]).then_inc(s["out_done"], 16)
                sp.wait_ge(s["out_done"], 16 * 2)
            with sp.Else():
                for t in range(S):
                    sp.wait_ge(s["acc_done"], S * (E - 1) + t + 1)
                    sp.dma_start(out[t], acc[:, (E - 1) % 2, t]).then_inc(s["out_done"], 16)
                sp.wait_ge(s["out_done"], 16 * S)

        @block.gpsimd
        def _(pool):
            g = nc.gpsimd
            g.memset(bqkv[:], 0.0).then_inc(s["bqkv_zeroed"], 1)
            g.memset(ident[:], 0.0).then_inc(s["ident_zeroed"], 1)
            pool.wait_ge(s["ident_zeroed"], 1)
            g.affine_select(out=ident[:], in_=ident[:], compare_op=ALU.not_equal, fill=1.0, base=0,
                            pattern=[[-1, 128]], channel_multiplier=1).then_inc(s["ident_done"], 1)
            g.memset(ones[:], 1.0).then_inc(s["ones_done"], 1)
            pool.wait_ge(s["ident_done"], 1)
            g.tensor_copy(ident_b[:], ident[:]).then_inc(s["ident_b_done"], 1)
            g.memset(half[:], -0.5).then_inc(s["half_done"], 1)
            g.memset(ones_b[:], 1.0).then_inc(s["ones_b_done"], 1)
            pool.wait_ge(s["ones_b_done"], 1)
            g.affine_select(out=tri_b[:], in_=ones_b[:], compare_op=ALU.is_gt, fill=0.0, base=0,
                            pattern=[[1, 128]], channel_multiplier=-1).then_inc(s["tri_done"], 1)
            g.iota(iota_e[:], pattern=[[1, E]], base=0, channel_multiplier=0,
                   allow_small_or_imprecise_dtypes=True).then_inc(s["iota_done"], 1)
            pool.wait_ge(s["half_done"], 1)
            pool.wait_ge(s["var_eps_done"], 1)
            for i in range(2):
                g.tensor_tensor(rstd[0][:, 2 * i:2 * i + 2], var_eps[0][:, 2 * i:2 * i + 2], half[:, 0:2], ALU.pow).then_inc(s["rstd_done"], 1)
            pool.wait_ge(s["route_in"], 32)
            g.tensor_copy(idx_f[:], idx_sb[:]).then_inc(s["idx_done"], 1)
            g.memset(mask[:], 0.0).then_inc(s["mask_zeroed"], 1)
            pool.wait_ge(s["mask_zeroed"], 1)
            g.affine_select(out=mask[:], in_=mask[:], compare_op=ALU.is_ge, fill=BIG, base=0,
                            pattern=[[0, XH], [-1, B]], channel_multiplier=1).then_inc(s["mask_done"], 1)
            g.iota(slot_no[:], pattern=[[1, CAP], [0, E]], base=0, channel_multiplier=0,
                   allow_small_or_imprecise_dtypes=True).then_inc(s["slot_done"], 1)
            pool.wait_ge(s["x_in"], 16)
            pool.wait_ge(s["rows_in"], 16)
            g.tensor_tensor(xbp[:], x_sb[:], row_sb[:, 0, :].rearrange("p (o d) -> p o d", o=1).to_broadcast([128, S, D]),
                            ALU.add).then_inc(s["xbp_done"], 1)
            g.memset(tor[:], 0.0).then_inc(s["tor_zeroed"], 1)
            pool.wait_ge(s["tor_zeroed"], 1)
            for i in range(S):
                for j in range(S):
                    n = (i == j) + ((i + 1) % S == j) + ((i - 1) % S == j)
                    if n:
                        g.memset(tor[:, i, j:j + 1], float(n)).then_inc(s["tor_done"], 1)
            pool.wait_ge(s["pick_done"], TOPK)
            for j in range(TOPK):
                g.tensor_tensor(pick_w[:, j], pick[:, j], wt_sb[:, :, j:j + 1].to_broadcast([128, S, E]), ALU.mult).then_inc(s["pickw_done"], 1)
            pool.wait_ge(s["pickw_done"], TOPK)
            g.tensor_tensor(gate[:], pick_w[:, 0], pick_w[:, 1], ALU.add).then_inc(s["gate_done"], 1)
            pool.wait_ge(s["gate_done"], 1)
            g.tensor_copy(gate3[:, :, 0], gate[:]).then_inc(s["gate_hi"], 1)
            pool.wait_ge(s["gate_hi"], 1)
            g.tensor_tensor(gate_r[:, 0], gate[:], gate3[:, :, 0], ALU.subtract).then_inc(s["gate_rest"], 1)
            pool.wait_ge(s["gate_rest"], 1)
            g.tensor_copy(gate3[:, :, 1], gate_r[:, 0]).then_inc(s["gate_mid"], 1)
            pool.wait_ge(s["gate_mid"], 1)
            g.tensor_tensor(gate_r[:, 1], gate_r[:, 0], gate3[:, :, 1], ALU.subtract).then_inc(s["gate_rest2"], 1)
            pool.wait_ge(s["gate_rest2"], 1)
            g.tensor_copy(gate3[:, :, 2], gate_r[:, 1]).then_inc(s["gate3_done"], 1)
            for t in range(S):
                pool.wait_ge(s["var_eps_done"], 2 + t)
                g.tensor_tensor(rstd[1][:, t:t + 1], var_eps[1][:, t:t + 1], half[:, 0:1], ALU.pow).then_inc(s["rstd_done"], 1)
            for t in range(1, S):
                pool.wait_ge(s["qkv_done"], t + 1)
                g.tensor_tensor(qk[:, 0:t, t], qkv[:, 0:t, 0], qkv[:, t:t + 1, 1].to_broadcast([128, t, D]), ALU.mult).then_inc(s["qk_pool"], 1)
            pool.wait_ge(s["qk_pool"], S - 1)
            by_head = qk[:, 0:S - 1, S - 1].rearrange("p q (h d) -> p q h d", d=HD)
            g.tensor_tensor(head4[:], by_head[:, :, :, 0:4], by_head[:, :, :, 4:8], ALU.add).then_inc(s["head4_done"], 1)
            pool.wait_ge(s["head4_done"], 1)
            g.tensor_tensor(head2[:], head4[:, :, :, 0:2], head4[:, :, :, 2:4], ALU.add).then_inc(s["head2_done"], 1)
            pool.wait_ge(s["head2_done"], 1)
            g.tensor_tensor(sc0[:, 0:S - 1, S - 1], head2[:, :, :, 0], head2[:, :, :, 1], ALU.add).then_inc(s["sc0_pool"], 1)
            g.tensor_tensor(x1b[:], x1[:], row_sb[:, 1, :].rearrange("p (o d) -> p o d", o=1).to_broadcast([128, S, D]),
                            ALU.add).then_inc(s["x1b_done"], 1)
            t = S - 1
            q = slice(2, 4)
            pool.wait_ge(s["expr_done"], 2)
            g.tensor_tensor(pn[:, q], expd[:, q], expr[:, q].rearrange("p q (o h) -> p q o h", o=1).to_broadcast([128, 2, S, H]),
                            ALU.mult).then_inc(s["pn_pool"], 1)
            pool.wait_ge(s["pn_pool"], 1)
            g.tensor_tensor(pv[:, t].rearrange("p k (h d) -> p k h d", d=HD),
                            pn[:, t].rearrange("p k (h o) -> p k h o", o=1).to_broadcast([128, S, H, HD]),
                            qkv[:, :, 2].rearrange("p k (h d) -> p k h d", d=HD), ALU.mult).then_inc(s["pv_pool"], 1)
            pool.wait_ge(s["pv_pool"], 1)
            g.tensor_tensor(pv2[:, t], pv[:, t, 0:2], pv[:, t, 2:4], ALU.add).then_inc(s["pv2_pool"], 1)
            for t in range(S):
                pool.wait_ge(s["var_eps_done"], 2 + S + t)
                g.tensor_tensor(rstd[2][:, t:t + 1], var_eps[2][:, t:t + 1], half[:, 0:1], ALU.pow).then_inc(s["rstd_done"], 1)
            g.tensor_tensor(x2b[:], x2[:], row_sb[:, 2, :].rearrange("p (o d) -> p o d", o=1).to_broadcast([128, S, D]),
                            ALU.add).then_inc(s["x2b_done"], 1)

        @block.scalar
        def _(act):
            a = nc.scalar
            act.dma_start(wc_sb[:], w_cross).then_inc(s["wc_in"], 16)
            a.preload_act_table(ACT.Exp)
            for h in range(XH):
                act.wait_ge(s["fold_ps"], h + 1)
                for n in range(2):
                    a.activation(fold_sb[:, n, h], bank[FOLD_BANK[h]][:, n * D:(n + 1) * D], ACT.Copy).then_inc(s["fold_done"], 1)
            for h in range(XH):
                act.wait_ge(s["kq_ps"], h + 1)
                a.activation(kq_sb[:, :, h, :], bank[KQ_BANK[h]][:].rearrange("p (s k) -> p s k", s=S), ACT.Copy,
                             scale=-float(DK) ** -0.5).then_inc(s["kq_done"], 1)
            act.wait_ge(s["vp_ps"], 1)
            a.activation(vp_sb[:, 0].rearrange("p h d -> p (h d)"), bank[VP_BANK[0]][:, 0:XH * D], ACT.Copy).then_inc(s["vp_done"], 1)

            def exponential(t, h):
                act.wait_ge(s["score_done"], XH * t + h + 1)
                a.activation(prob[:, t, h], nscore[:, t, h], ACT.Exp, bias=nmax[:, t, h:h + 1], scale=-1.0,
                             accum_out=psum_row[:, t, h:h + 1]).then_inc(s["exp_done"], 1)

            def probs_by_key(t):
                act.wait_ge(s["probT_ps"], t + 1)
                a.activation(probT[:, t].rearrange("p h k -> p (h k)"), bank[PROBT_BANK[t]][:, 0:XH * B],
                             ACT.Copy).then_inc(s["probT_done"], 1)

            for t in range(S):
                exponential(t, 0)
                if t:
                    probs_by_key(t - 1)
                exponential(t, 1)
                if t == S - 2:
                    act.wait_ge(s["vp_ps"], S)
                    a.activation(vp_sb[:, S - 1].rearrange("p h d -> p (h d)"), bank[VP_BANK[S - 1]][:, 0:XH * D], ACT.Copy)\
                        .then_inc(s["vp_done"], 1)
                    act.wait_ge(s["wqkv_ps"], 1)
                    a.activation(wqkv_sb[:].rearrange("p a d -> p (a d)"), bank[WQKV_BANK][:, 0:3 * D], ACT.Copy).then_inc(s["wqkv_done"], 1)
            act.wait_ge(s["bqkv_ps"], 1)
            a.activation(bqkv[0:1, :], bank[BQKV_BANK][0:1, 0:3 * D], ACT.Copy).then_inc(s["bqkv_done"], 1)
            probs_by_key(S - 1)

            def turned(k):
                act.wait_ge(s["turn_ps"], k + 1)
                a.activation(takeT[:, k], bank[TURN_BANK[k % 2]][:], ACT.Copy).then_inc(s["turn_done"], 1)

            def xn_by_feature(t):
                act.wait_ge(s["xnT_ps"], 1 + t + 1)
                a.activation(xnT[1][:, t], bank[XNT1_BANK[t]][:, 0:B], ACT.Copy).then_inc(s["xnT_done"], 1)

            xn_by_feature(0)
            for t in range(1, S + 1):
                if t < S:
                    xn_by_feature(t)
                act.wait_ge(s["qkv_ps"], t)
                a.activation(qkv[:, t - 1].rearrange("p a d -> p (a d)"), bank[QKV_BANK[t - 1]][:, 0:3 * D], ACT.Copy)\
                    .then_inc(s["qkv_done"], 1)
            for k in range(TURNS):
                turned(k)
            for i in range(2):
                act.wait_ge(s["scd_done"], i + 1)
                a.activation(expd[:, 2 * i:2 * i + 2].rearrange("p q k h -> p (q k h)"),
                             scd[:, 2 * i:2 * i + 2].rearrange("p q k h -> p (q k h)"), ACT.Exp).then_inc(s["expd_done"], 1)
            for k in range(TURNS, SC):
                turned(k)
            for t in range(S):
                act.wait_ge(s["oT_ps"], t + 1)
                a.activation(oT[:, t], bank[OT_BANK[t]][:, 0:B], ACT.Copy).then_inc(s["oT_done"], 1)
            for t in range(S):
                act.wait_ge(s["xn_done"], 2 * S + t + 1)
                a.activation(xn3[:, t, 0], xn[2][:, t], ACT.Copy).then_inc(s["xn3_hi"], 1)
                act.wait_ge(s["xn3_rest"], t + 1)
                a.activation(xn3[:, t, 1], xn3_r[:, t], ACT.Copy).then_inc(s["xn3_mid"], 1)
            a.preload_act_table(ACT.Gelu)
            act.wait_ge(s["most_done"], 1)
            fullest = act.alloc_register("fullest_for_act")
            act.reg_load(fullest, most[0:1, 0:1])
            with act.If_lt(fullest, LIMIT + 1):
                def gelu(e, c):
                    if e >= 2:
                        act.wait_ge(s["yT_ps"], e - 1)
                    act.wait_ge(s["hr_ps"], 2 * e + c + 1)
                    a.activation(hidr[:, e % 2, 2 * c:2 * c + 2], bank[HR_BANK[e][c]][:, 0:2 * CAP].rearrange("p (c n) -> p c n", c=2),
                                 ACT.Gelu).then_inc(s["hr_done"], 1)

                def part_hi(k):
                    if k >= 3:
                        act.wait_ge(s["scatter_done"], k - 2)
                    act.wait_ge(s["ys_done"], k + 1)
                    a.activation(ys3[:, k % 3, 0], ys[:, k % 3], ACT.Copy).then_inc(s["ys_hi"], 1)

                def part_mid(k):
                    act.wait_ge(s["ys_rest"], k + 1)
                    a.activation(ys3[:, k % 3, 1], ysr[:, k % 3], ACT.Copy).then_inc(s["ys_mid"], 1)

                act.wait_ge(s["xg_ps"], 2)
                a.activation(xg[:, 3 * CAP:6 * CAP], bank[GATHER_BANK[1]][:, 0:3 * CAP], ACT.Copy).then_inc(s["xg_act"], 1)
                for e in range(E):
                    if e >= 2:
                        part_hi(e - 2)
                    gelu(e, 0)
                    if e >= 2:
                        part_mid(e - 2)
                    gelu(e, 1)
                part_hi(SC - 3)
                part_mid(SC - 3)
                for step in (part_hi, part_mid):
                    step(SC - 2)
                    step(SC - 1)
            with act.Else():
                for t in range(S):
                    act.wait_ge(s["xnT_ps"], 1 + S + t + 1)
                    a.activation(xnT[2][:, t], bank[XNT2_BANK[t]][:, 0:B], ACT.Copy).then_inc(s["xnT_done"], 1)
                for e in range(E):
                    if e >= 2:
                        act.wait_ge(s["y_ps"], S * (e - 1))
                    for c in range(FC):
                        act.wait_ge(s["h_ps"], FC * e + c + 1)
                        a.activation(hid[:, e % 2, c], bank[H_BANK[c]][:], ACT.Gelu).then_inc(s["h_done"], 1)

        @block.vector
        def _(dve):
            v = nc.vector

            v.memset(warm[:], 0.0).then_inc(s["warm_done"], 1)
            v.memset(picked[:], 0.0).then_inc(s["picked_zeroed"], 1)
            dve.wait_ge(s["ident_done"], 1)
            v.tensor_reduce(owner[:], ident[:].rearrange("p (n e) -> p e n", e=E), AX.X, ALU.add).then_inc(s["owner_done"], 1)
            dve.wait_ge(s["x_in"], 16)
            for t in range(S):
                v.bn_stats(stats[0][:, t], x_sb[:, t]).then_inc(s["stats_done"], 1)
            for t in range(S):
                dve.wait_ge(s["stats_done"], t + 1)
                v.bn_aggr(mv[0][:, t], stats[0][:, t]).then_inc(s["mv_done"], 1)
            dve.wait_ge(s["mv_done"], S)
            v.tensor_scalar(var_eps[0][:], mv[0][:, :, 1], EPS, None, ALU.add).then_inc(s["var_eps_done"], 1)
            for t in range(S):
                dve.wait_ge(s["rstd_done"], t // 2 + 1)
                v.tensor_scalar(xn[0][:, t], x_sb[:, t], mv[0][:, t, 0:1], rstd[0][:, t:t + 1], ALU.subtract,
                                ALU.mult).then_inc(s["xn_done"], 1)
            dve.wait_ge(s["idx_done"], 1)
            dve.wait_ge(s["iota_done"], 1)
            for j in range(TOPK):
                v.tensor_tensor(pick[:, j], idx_f[:, :, j:j + 1].to_broadcast([128, S, E]),
                                iota_e[:].rearrange("p (o e) -> p o e", o=1).to_broadcast([128, S, E]),
                                ALU.is_equal).then_inc(s["pick_done"], 1)
            dve.wait_ge(s["pick_done"], TOPK)
            dve.wait_ge(s["picked_zeroed"], 1)
            v.tensor_tensor(picked[:, 0:S], pick[:, 0], pick[:, 1], ALU.max).then_inc(s["picked_done"], 1)
            dve.wait_ge(s["xnT_ps"], 1)
            for i in range(2):
                v.tensor_copy(xnT[0][:, 2 * i:2 * i + 2].rearrange("p s b -> p (s b)"), bank[XNT_BANK][:, 2 * i * B:(2 * i + 2) * B])\
                    .then_inc(s["xnT0_done"], 1)
            dve.wait_ge(s["rank_ps"], 1)
            v.scalar_tensor_tensor(out=code0[:], in0=picked[:, 0:S], scalar=-CODE,
                                   in1=bank[RANK_BANK][:, 0:S * E].rearrange("p (t e) -> p t e", e=E),
                                   op0=ALU.mult, op1=ALU.add).then_inc(s["code_done"], 1)
            v.tensor_reduce(most[:], bank[RANK_BANK][:, S * E:(S + 1) * E], AX.X, ALU.max).then_inc(s["most_done"], 1)
            dve.wait_ge(s["code_done"], 1)
            v.tensor_scalar(code[:], code0[:], CODE, None, ALU.add).then_inc(s["code_done"], 1)

            dve.wait_ge(s["mask_done"], 1)
            for t in range(S):
                dve.wait_ge(s["score_ps"], t + 1)
                for h in range(XH):
                    v.tensor_tensor_reduce(out=nscore[:, t, h], in0=bank[SCORE_BANK[t]][:, h * B:(h + 1) * B], in1=mask[:, h],
                                           scale=1.0, scalar=3.0e38, op0=ALU.add, op1=ALU.min,
                                           accum_out=nmax[:, t, h:h + 1]).then_inc(s["score_done"], 1)

            def slots_taken(t):
                dve.wait_ge(s["slot_done"], 1)
                dve.wait_ge(s["code_done"], 2)
                v.tensor_tensor(take[:, t], slot_no[:], code[:, t:t + 1].to_broadcast([128, CAP, E]),
                                ALU.is_equal).then_inc(s["take_done"], 1)

            slots_taken(0)
            dve.wait_ge(s["vp_ps"], 3)
            v.tensor_copy(vp_sb[:, 1:3].rearrange("p s h d -> p (s h d)"), bank[VP_BANK[1]][:]).then_inc(s["vp_mid_done"], 1)

            def row_sums(t):
                dve.wait_ge(s["exp_done"], XH * (t + 1))
                v.reciprocal(rsum[:, t], psum_row[:, t]).then_inc(s["rsum_done"], 1)

            def residual_a(t):
                dve.wait_ge(s["rsum_done"], t + 1)
                dve.wait_ge(s["xo_ps"], t + 1)
                v.scalar_tensor_tensor(out=x1a[:, t], in0=bank[XO_BANK[t]][:, 0:D], scalar=rsum[:, t, 0:1], in1=xbp[:, t],
                                       op0=ALU.mult, op1=ALU.add).then_inc(s["x1a_done"], 1)

            def residual_b(t):
                dve.wait_ge(s["x1a_done"], t + 1)
                v.scalar_tensor_tensor(out=x1[:, t], in0=bank[XO_BANK[t]][:, D:2 * D], scalar=rsum[:, t, 1:2],
                                       in1=x1a[:, t], op0=ALU.mult, op1=ALU.add).then_inc(s["x1_done"], 1)

            def norm_stats(n, src, ready, t):
                dve.wait_ge(s[ready], t + 1)
                v.bn_stats(stats[n][:, t], src[:, t]).then_inc(s["stats_done"], 1)

            def norm_mv(n, t):
                dve.wait_ge(s["stats_done"], n * S + t + 1)
                v.bn_aggr(mv[n][:, t], stats[n][:, t]).then_inc(s["mv_done"], 1)

            def norm_eps(n, t):
                dve.wait_ge(s["mv_done"], n * S + t + 1)
                v.tensor_scalar(var_eps[n][:, t:t + 1], mv[n][:, t, 1:2], EPS, None, ALU.add).then_inc(s["var_eps_done"], 1)

            def norm_apply(n, src, t):
                dve.wait_ge(s["rstd_done"], 2 + (n - 1) * S + t + 1)
                v.tensor_scalar(xn[n][:, t], src[:, t], mv[n][:, t, 0:1], rstd[n][:, t:t + 1], ALU.subtract,
                                ALU.mult).then_inc(s["xn_done"], 1)

            def products(t):
                dve.wait_ge(s["qkv_done"], t + 1)
                v.tensor_tensor(qk[:, t, 0:t + 1], qkv[:, t:t + 1, 0].to_broadcast([128, t + 1, D]), qkv[:, 0:t + 1, 1],
                                ALU.mult).then_inc(s["qk_done"], 1)

            def head_sums(t):
                dve.wait_ge(s["qk_done"], t + 1)
                v.tensor_reduce(sc0[:, t, 0:t + 1], qk[:, t, 0:t + 1].rearrange("p k (h d) -> p k h d", d=HD), AX.X,
                                ALU.add).then_inc(s["sc0_done"], 1)
                if 0 < t < S - 1:
                    dve.wait_ge(s["qk_pool"], t)
                    v.tensor_reduce(sc0[:, 0:t, t], qk[:, 0:t, t].rearrange("p q (h d) -> p q h d", d=HD), AX.X,
                                    ALU.add).then_inc(s["sc0_done"], 1)

            dve.wait_ge(s["rows_in"], 16)
            dve.wait_ge(s["xbp_done"], 1)
            for w in range(S + 1):
                if w < S:
                    row_sums(w)
                if w:
                    norm_mv(1, w - 1)
                if w < S:
                    residual_a(w)
                if w:
                    norm_eps(1, w - 1)
                if w < S:
                    residual_b(w)
                    norm_stats(1, x1, "x1_done", w)
                if w == S:
                    slots_taken(1)
                if w:
                    norm_apply(1, x1, w - 1)
            for t in range(S):
                products(t)
                if t < 2:
                    slots_taken(2 + t)
                if t:
                    head_sums(t - 1)
            head_sums(S - 1)

            def wide(ap):
                return ap.rearrange("p q (o h) -> p q o h", o=1).to_broadcast([128, 2, S, H])

            def halves(step):
                for i in range(2):
                    step(i, slice(2 * i, 2 * i + 2))

            def add_toroidal(i, q):
                dve.wait_ge(s["tor_done"], 3 * S)
                dve.wait_ge(s["sc0_done"], 2 * S - 2)
                dve.wait_ge(s["sc0_pool"], 1)
                v.scalar_tensor_tensor(out=sc[:, q].rearrange("p q k h -> p (q k) h"), in0=sc0[:, q].rearrange("p q k h -> p (q k) h"),
                                       scalar=QSCALE, in1=tor[:, q].rearrange("p q (k o) -> p (q k) o", o=1).to_broadcast([128, 2 * S, H]),
                                       op0=ALU.mult, op1=ALU.add).then_inc(s["sc_done"], 1)

            def row_max(i, q):
                dve.wait_ge(s["sc_done"], i + 1)
                v.tensor_reduce(scm[:, q], sc[:, q].rearrange("p q k h -> p q h k"), AX.X, ALU.max).then_inc(s["scm_done"], 1)

            def less_max(i, q):
                dve.wait_ge(s["scm_done"], i + 1)
                v.tensor_tensor(scd[:, q], sc[:, q], wide(scm[:, q]), ALU.subtract).then_inc(s["scd_done"], 1)

            def exp_sum(i, q):
                dve.wait_ge(s["expd_done"], i + 1)
                v.tensor_reduce(exps[:, q], expd[:, q].rearrange("p q k h -> p q h k"), AX.X, ALU.add).then_inc(s["exps_done"], 1)

            def inverse(i, q):
                dve.wait_ge(s["exps_done"], i + 1)
                v.reciprocal(expr[:, q], exps[:, q]).then_inc(s["expr_done"], 1)

            def probabilities(i, q):
                dve.wait_ge(s["expr_done"], i + 1)
                v.tensor_tensor(pn[:, q], expd[:, q], wide(expr[:, q]), ALU.mult).then_inc(s["pn_done"], 1)

            for step in (add_toroidal, row_max, less_max, exp_sum, inverse):
                halves(step)
            probabilities(0, slice(0, 2))

            def weigh_values(q, k0, k1):
                dve.wait_ge(s["pn_done" if q < 2 else "pn_pool"], 1)
                v.tensor_tensor(pv[:, q, k0:k1].rearrange("p k (h d) -> p k h d", d=HD),
                                pn[:, q, k0:k1].rearrange("p k (h o) -> p k h o", o=1).to_broadcast([128, k1 - k0, H, HD]),
                                qkv[:, k0:k1, 2].rearrange("p k (h d) -> p k h d", d=HD), ALU.mult).then_inc(s["pv_done"], 1)

            def add_pairs(q):
                dve.wait_ge(s["pv_done"], q + 2)
                v.tensor_tensor(pv2[:, q], pv[:, q, 0:2], pv[:, q, 2:4], ALU.add).then_inc(s["pv2_done"], 1)

            weigh_values(0, 0, 2)
            weigh_values(0, 2, S)
            weigh_values(1, 0, S)
            weigh_values(2, 0, S)
            add_pairs(1)
            add_pairs(2)
            dve.wait_ge(s["owner_done"], 1)
            dve.wait_ge(s["gates_ps"], 1)
            v.tensor_tensor(shared[:], bank[GATE_BANK][:, 3 * E:6 * E].rearrange("p (g e) -> p g e", g=3),
                            owner[:].rearrange("p (o e) -> p o e", o=1).to_broadcast([128, 3, E]), ALU.mult)\
                .then_inc(s["gates_read"], 1)
            dve.wait_ge(s["x1b_done"], 1)

            def residual_2(t):
                dve.wait_ge(s["so_ps"], t + 1)
                v.tensor_tensor(x2[:, t], bank[SO_BANK[t]][:, 0:D], x1b[:, t], ALU.add).then_inc(s["x2_done"], 1)

            def split_rest(t):
                dve.wait_ge(s["xn3_hi"], t + 1)
                v.tensor_tensor(xn3_r[:, t], xn[2][:, t], xn3[:, t, 0], ALU.subtract).then_inc(s["xn3_rest"], 1)

            def split_low(t):
                dve.wait_ge(s["xn3_mid"], t + 1)
                v.tensor_tensor(xn3[:, t, 2], xn3_r[:, t], xn3[:, t, 1], ALU.subtract).then_inc(s["xn3_lo"], 1)

            for w in range(S + 3):
                if 0 < w <= S:
                    norm_mv(2, w - 1)
                if w < S and w != 1:
                    residual_2(w)
                if 0 < w <= S:
                    norm_eps(2, w - 1)
                if w == 1:
                    residual_2(1)
                if w == 0:
                    v.tensor_reduce(slot_gate[:, 0:E], bank[GATE_BANK][:, 0:3 * E].rearrange("p (k g) -> p k g", g=3), AX.X, ALU.add)\
                        .then_inc(s["gates_read"], 1)
                if 1 < w <= S + 1:
                    split_rest(w - 2)
                if w > 2:
                    split_low(w - 3)
                if w < S:
                    norm_stats(2, x2, "x2_done", w)
                if w == 0:
                    dve.wait_ge(s["gates_read"], 2)
                    v.tensor_reduce(slot_gate[:, E:SC], shared[:], AX.XY, ALU.add).then_inc(s["slot_gate_done"], 1)
                if 0 < w <= S:
                    norm_apply(2, x2, w - 1)
            dve.wait_ge(s["most_done"], 1)
            fullest = dve.alloc_register("fullest_for_dve")
            dve.reg_load(fullest, most[0:1, 0:1])
            with dve.If_lt(fullest, LIMIT + 1):
                for n, lo, hi in ((0, 0, 1), (0, 1, 3), (2, 6, E)):
                    dve.wait_ge(s["xg_ps"], n + 1)
                    v.tensor_copy(xg[:, lo * CAP:hi * CAP], bank[GATHER_BANK[n]][:, (lo - 3 * n) * CAP:(hi - 3 * n) * CAP])\
                        .then_inc(s["xg_done"], 1)

                def by_feature(e):
                    dve.wait_ge(s["yT_ps"], e + 1)
                    v.tensor_copy(yT[:, :, e], bank[YT_BANK][:, 0:CAP]).then_inc(s["yT_done"], 1)

                def gated(k):
                    dve.wait_ge(s["ys_ps"], k + 1)
                    v.tensor_scalar(ys[:, k % 3], bank[YS_BANK[k]][:, 0:D], slot_gate[:, k:k + 1], None, ALU.mult).then_inc(s["ys_done"], 1)

                def gated_rest(k):
                    dve.wait_ge(s["ys_hi"], k + 1)
                    v.tensor_tensor(ysr[:, k % 3], ys[:, k % 3], ys3[:, k % 3, 0], ALU.subtract).then_inc(s["ys_rest"], 1)

                def gated_low(k):
                    dve.wait_ge(s["ys_mid"], k + 1)
                    v.tensor_tensor(ys3[:, k % 3, 2], ysr[:, k % 3], ys3[:, k % 3, 1], ALU.subtract).then_inc(s["ys_lo"], 1)

                steps = (gated, gated_rest, gated_low)
                dve.wait_ge(s["slot_gate_done"], 1)
                for e in range(E - 1):
                    by_feature(e)
                    if e < E - 2:
                        for step in steps:
                            step(e)
                gated(SC - 3)
                gated_rest(SC - 3)
                by_feature(E - 1)
                gated_low(SC - 3)
                for step in steps:
                    step(SC - 2)
                    step(SC - 1)
                dve.wait_ge(s["x2b_done"], 1)
                for t in range(S):
                    dve.wait_ge(s["sum_ps"], t + 1)
                    v.tensor_tensor(res[:, t], bank[SUM_BANK[t]][:, 0:D], x2b[:, t], ALU.add).then_inc(s["res_done"], 1)
            with dve.Else():
                dve.wait_ge(s["gate_done"], 1)
                dve.wait_ge(s["x2b_done"], 1)
                for e in range(E):
                    for t in range(S):
                        dve.wait_ge(s["y_ps"], S * e + t + 1)
                        if e:
                            dve.wait_ge(s["acc_done"], S * (e - 1) + t + 1)
                        v.scalar_tensor_tensor(out=acc[:, e % 2, t], in0=bank[Y_BANK[t]][:, 0:D],
                                               scalar=gate[:, t, e:e + 1], in1=acc[:, (e - 1) % 2, t] if e else x2b[:, t],
                                               op0=ALU.mult, op1=ALU.add).then_inc(s["acc_done"], 1)

        @block.tensor
        def _(pe):
            mm, tr = nc.tensor.matmul, nc.tensor.transpose
            zero = nc.const_aps.tensor(0.0, [128, 512], F32)

            def keep_warm(n):
                for _ in range(n):
                    mm(bank[WARM_BANK][:], warm[:, 0:128], warm[:], start=True, stop=True)

            for n in FIRST_WARM:
                mm(bank[SCORE_BANK[0]][0:32, 0:n], zero[:, 0:32], zero[:, 0:n], start=True, stop=True)
            pe.wait_ge(s["wc_in"], 16)
            for h in range(XH):
                r = slice(h * DK, (h + 1) * DK)
                for n in range(2):
                    last = mm(bank[FOLD_BANK[h]][:, n * D:(n + 1) * D], wc_sb[r, 1 + n, :], wc_sb[r, 3 * n, :], start=True, stop=True)
                last.then_inc(s["fold_ps"], 1)

            def keys(h):
                pe.wait_ge(s["fold_done"], 2 * h + 1)
                mm(bank[KQ_BANK[h]][:], fold_sb[:, 0, h], ctx_sb[:].rearrange("p s k -> p (s k)"), start=True, stop=True).then_inc(s["kq_ps"], 1)

            def values(t):
                first = (t == 2) * XH * D
                mm(bank[VP_BANK[t]][:, first:first + XH * D], ctx_sb[:, t], fold_sb[:, 1].rearrange("p h d -> p (h d)"),
                   start=True, stop=True).then_inc(s["vp_ps"], 1)

            pe.wait_ge(s["ctx_in"], 16)
            keys(0)
            keys(1)
            pe.wait_ge(s["ident_done"], 1)
            for t in range(S):
                pe.wait_ge(s["xn_done"], t + 1)
                last = tr(bank[XNT_BANK][:, t * B:(t + 1) * B], xn[0][:, t], ident[:])
            last.then_inc(s["xnT_ps"], 1)
            pe.wait_ge(s["fold_done"], 2 * XH)
            pe.wait_ge(s["picked_done"], 1)
            pe.wait_ge(s["tri_done"], 1)
            mm(bank[RANK_BANK][:, 0:(S + 1) * E], tri_b[:], picked[:].rearrange("p t e -> p (t e)"), start=True, stop=False)
            for t in range(S):
                last = mm(bank[RANK_BANK][:, (t + 1) * E:(S + 1) * E], ones_b[:],
                          picked[:, t:t + 1].to_broadcast([128, S - t, E]), start=False, stop=(t == S - 1))
            last.then_inc(s["rank_ps"], 1)
            values(0)
            pe.wait_ge(s["kq_done"], 2)
            for t in range(S):
                pe.wait_ge(s["xnT0_done"], 1 if t == 0 else 2)
                mm(bank[SCORE_BANK[t]][:, 0:XH * B], xnT[0][:, t], kq_sb[:, t].rearrange("p h k -> p (h k)"),
                   start=True, stop=True).then_inc(s["score_ps"], 1)

            def probs_turned(t):
                pe.wait_ge(s["score_done"], XH * (t + 1))
                for h in range(XH):
                    pe.wait_ge(s["exp_done"], XH * t + h + 1)
                    last = tr(bank[PROBT_BANK[t]][:, h * B:(h + 1) * B], prob[:, t, h], ident[:])
                last.then_inc(s["probT_ps"], 1)

            def probs_out(t):
                pe.wait_ge(s["probT_done"], t + 1)
                if t in (1, 2):
                    pe.wait_ge(s["vp_mid_done"], 1)
                else:
                    pe.wait_ge(s["vp_done"], 2 if t == S - 1 else 1)
                for h in range(XH):
                    last = mm(bank[XO_BANK[t]][:, h * D:(h + 1) * D], probT[:, t, h], vp_sb[:, t, h], start=True, stop=True)
                last.then_inc(s["xo_ps"], 1)

            values(1)
            probs_turned(0)
            values(2)
            probs_out(0)
            probs_turned(1)
            values(3)
            pe.wait_ge(s["ws_in"], 16)
            pe.wait_ge(s["most_done"], 1)
            mm(bank[WQKV_BANK][:, 0:3 * D], ws_sb[:, 0], ws_sb[:, 1:4].rearrange("p a d -> p (a d)"), start=True, stop=True).then_inc(s["wqkv_ps"], 1)
            probs_out(1)
            probs_turned(2)
            pe.wait_ge(s["bias_in"], 32)
            pe.wait_ge(s["vp_done"], 2)
            mm(bank[BQKV_BANK][0:1, 0:3 * D], btor_sb[:], ws_sb[:, 1:4].rearrange("p a d -> p (a d)"), start=True, stop=True)\
                .then_inc(s["bqkv_ps"], 1)
            probs_out(2)
            probs_turned(3)

            def transpose_1(t):
                pe.wait_ge(s["xn_done"], S + t + 1)
                tr(bank[XNT1_BANK[t]][:, 0:B], xn[1][:, t], ident[:]).then_inc(s["xnT_ps"], 1)

            def chunk(t, k):
                return take[:, t, 0:CHUNK, k] if k < E else take[:, t, CHUNK:CAP].rearrange("p n e -> p (n e)")

            def turn(k):
                if k > 1:
                    pe.wait_ge(s["turn_done"], k - 1)
                for t in range(S):
                    if k == 0:
                        pe.wait_ge(s["take_done"], t + 1)
                    last = mm(bank[TURN_BANK[k % 2]][:, t * B:(t + 1) * B], chunk(t, k), ident_b[:], start=True, stop=True)
                last.then_inc(s["turn_ps"], 1)

            def bias_1(t):
                if t == 2:
                    pe.wait_ge(s["xnT_done"], 1)
                elif t == 3:
                    pe.wait_ge(s["x1_done"], XO_BANK.index(QKV_BANK[3]) + 1)
                mm(bank[QKV_BANK[t]][:, 0:3 * D], ones[:], bqkv[:], start=True, stop=False)

            def project(t):
                pe.wait_ge(s["xnT_done"], t + 1)
                mm(bank[QKV_BANK[t]][:, 0:3 * D], xnT[1][:, t], wqkv_sb[:].rearrange("p a d -> p (a d)"), start=False, stop=True)\
                    .then_inc(s["qkv_ps"], 1)

            transpose_1(0)
            pe.wait_ge(s["ones_done"], 1)
            pe.wait_ge(s["wqkv_done"], 1)
            pe.wait_ge(s["bqkv_done"], 1)
            bias_1(0)
            probs_out(S - 1)
            project(0)
            for t in range(1, S):
                transpose_1(t)
                bias_1(t)
                project(t)

            def slot_gates_by_chunk():
                pe.wait_ge(s["gate3_done"], 1)
                for n in range(SC):
                    for t in range(S):
                        cols, gates = ((slice(3 * n, 3 * n + 3), gate3[:, t, :, n]) if n < E else
                                       (slice(3 * E, 6 * E), gate3[:, t].rearrange("p g e -> p (g e)")))
                        last = mm(bank[GATE_BANK][:, cols], chunk(t, n), gates, start=(t == 0), stop=(t == S - 1))
                last.then_inc(s["gates_ps"], 1)

            pe.wait_ge(s["warm_done"], 1)
            pe.wait_ge(s["ident_b_done"], 1)
            pe.wait_ge(s["xnT_done"], S)
            pe.wait_ge(s["qkv_done"], S)
            for k in range(SC):
                turn(k)
                if k == TURNS - 1:
                    slot_gates_by_chunk()
                else:
                    keep_warm(1)
            keep_warm(LAST_WARM)

            def summed(q):
                for k in range(S if q == 0 else S // 2):
                    if q == 0:
                        pe.wait_ge(s["pv_done"], k // 2 + 1)
                        term, last_k = pv[:, q, k], S - 1
                    else:
                        pe.wait_ge(s["pv2_pool"], 1) if q == S - 1 else pe.wait_ge(s["pv2_done"], q)
                        term, last_k = pv2[:, q, k], S // 2 - 1
                    last = mm(bank[OT_BANK[q]][:, 0:B], term, ident[:], start=(k == 0), stop=(k == last_k))
                last.then_inc(s["oT_ps"], 1)

            def through_out_w(q):
                pe.wait_ge(s["oT_done"], q + 1)
                if SO_BANK[q] == GATE_BANK:
                    pe.wait_ge(s["gates_read"], 2)
                mm(bank[SO_BANK[q]][:, 0:D], oT[:, q], ws_sb[:, 4], start=True, stop=True).then_inc(s["so_ps"], 1)

            summed(0)
            through_out_w(0)
            summed(1)
            summed(2)
            through_out_w(1)
            summed(3)
            through_out_w(2)
            through_out_w(S - 1)
            def gather(t, part):
                pe.wait_ge(s[("xn3_hi", "xn3_mid", "xn3_lo")[part]], t + 1)
                for n in range(3):
                    lo, hi = 3 * n, min(3 * (n + 1), E)
                    last = mm(bank[GATHER_BANK[n]][:, 0:(hi - lo) * CAP], xn3[:, t, part],
                              take[:, t, :, lo:hi].rearrange("p n e -> p e n"),
                              start=(t == 0 and part == 0), stop=(t == S - 1 and part == 2))
                    if t == S - 1 and part == 2:
                        last.then_inc(s["xg_ps"], 1)

            pe.wait_ge(s["turn_done"], SC)
            for w in range(S + 1):
                if w:
                    gather(w - 1, 1)
                if w < S:
                    gather(w, 0)
                if w:
                    gather(w - 1, 2)
            pe.wait_ge(s["most_done"], 1)
            fullest = pe.alloc_register("fullest_for_pe")
            pe.reg_load(fullest, most[0:1, 0:1])
            with pe.If_lt(fullest, LIMIT + 1):
                def hidden(e):
                    pe.wait_ge(w1_in[e // 2], 16)
                    if e == 0:
                        pe.wait_ge(s["x2_done"], S)
                    if 3 <= e < 6:
                        pe.wait_ge(s["xg_act"], 1)
                    else:
                        pe.wait_ge(s["xg_done"], 3 if e >= 6 else min(e + 1, 2))
                    for c in range(FC):
                        if e > 1 and c % 2 == 0:
                            before = max(d for d in range(e) if HR_BANK[d] == HR_BANK[e])
                            pe.wait_ge(s["hr_done"], 2 * before + c // 2 + 1)
                        last = mm(bank[HR_BANK[e][c // 2]][:, c % 2 * CAP:(c % 2 + 1) * CAP], w1_sb[:, e, c * 128:(c + 1) * 128],
                                  xg[:, e * CAP:(e + 1) * CAP], start=True, stop=True)
                        if c % 2:
                            last.then_inc(s["hr_ps"], 1)

                def expert_out(e):
                    pe.wait_ge(w2_in[e // 2], 16)
                    pe.wait_ge(s["hr_done"], 2 * (e + 1))
                    if e:
                        pe.wait_ge(s["yT_done"], e)
                    for c in range(FC):
                        last = mm(bank[YT_BANK][:, 0:CAP], w2_sb[:, e, c], hidr[:, e % 2, c], start=(c == 0), stop=(c == FC - 1))
                    last.then_inc(s["yT_ps"], 1)

                def by_slot(k):
                    pe.wait_ge(s["yT_done"], last_expert(k) + 1)
                    if k == 0:
                        pe.wait_ge(s["hr_done"], 2 * 2)
                    if 0 < k < SC - 1:
                        pe.wait_ge(s["ys_done"], k)
                    y = yT[:, 0:CHUNK, k] if k < E else yT[:, CHUNK:CAP].rearrange("p n e -> p (n e)")
                    tr(bank[YS_BANK[k]][:, 0:D], y, ident[:]).then_inc(s["ys_ps"], 1)

                def scatter(k, part):
                    if k == 0 and part == 0:
                        pe.wait_ge(s["xg_done"], 3)
                        pe.wait_ge(s["xg_act"], 1)
                    pe.wait_ge(s[("ys_hi", "ys_mid", "ys_lo")[part]], k + 1)
                    for t in range(S):
                        last = mm(bank[SUM_BANK[t]][:, 0:D], takeT[:, k, t * B:(t + 1) * B], ys3[:, k % 3, part],
                                  start=(k == 0 and part == 0), stop=(k == SC - 1 and part == 2))
                        if k == SC - 1 and part == 2:
                            last.then_inc(s["sum_ps"], 1)
                    if k < SC - 1 and part == 2:
                        last.then_inc(s["scatter_done"], 1)

                def scatter_all(k):
                    for part in range(3):
                        scatter(k, part)

                for e in range(E):
                    hidden(e)
                    if e:
                        expert_out(e - 1)
                        if e >= 2:
                            scatter_all(e - 2)
                        by_slot(e - 1)
                expert_out(E - 1)
                by_slot(SC - 2)
                by_slot(SC - 1)
                for k, part in ((SC - 3, 0), (SC - 3, 1), (SC - 3, 2), (SC - 2, 0), (SC - 1, 0), (SC - 2, 1), (SC - 1, 1),
                                (SC - 2, 2), (SC - 1, 2)):
                    scatter(k, part)
            with pe.Else():
                for t in range(S):
                    pe.wait_ge(s["xn_done"], 2 * S + t + 1)
                    tr(bank[XNT2_BANK[t]][:, 0:B], xn[2][:, t], ident[:]).then_inc(s["xnT_ps"], 1)
                pe.wait_ge(s["xnT_done"], 2 * S)
                pe.wait_ge(s["x2_done"], S)

                def hidden(e):
                    pe.wait_ge(w1_in[e // 2], 16)
                    for c in range(FC):
                        if e:
                            pe.wait_ge(s["h_done"], FC * (e - 1) + c + 1)
                        mm(bank[H_BANK[c]][:], w1_sb[:, e, c * 128:(c + 1) * 128], xnT[2][:].rearrange("p s b -> p (s b)"),
                           start=True, stop=True).then_inc(s["h_ps"], 1)

                def expert_out(e):
                    pe.wait_ge(w2_in[e // 2], 16)
                    pe.wait_ge(s["h_done"], FC * (e + 1))
                    for t in range(S):
                        if e:
                            pe.wait_ge(s["acc_done"], S * (e - 1) + t + 1)
                        for c in range(FC):
                            last = mm(bank[Y_BANK[t]][:, 0:D], hid[:, e % 2, c, t * B:(t + 1) * B], w2_sb[:, e, c],
                                      start=(c == 0), stop=(c == FC - 1))
                        last.then_inc(s["y_ps"], 1)

                for e in range(E):
                    hidden(e)
                    if e:
                        expert_out(e - 1)
                expert_out(E - 1)


_ORDER = ["x", "ctxT", "w_cross", "w_self", "cols", "in_bias", "rows", "exp_idx", "exp_wt", "w1", "w2"]


def kernel(x, ctx_1024, L0_xattn_Wq, L0_xattn_Wk, L0_xattn_Wv, L0_xattn_Wp, L0_xattn_bp, L0_attn_w_tor, L0_attn_b_tor,
           L0_attn_in_proj_w, L0_attn_in_proj_b, L0_attn_out_w, L0_attn_out_b, L0_ffn_scores, L0_ffn_expert_weights,
           L0_ffn_expert_indices, L0_ffn_w1, L0_ffn_w2, L0_ffn_bias):
    import numpy as np
    import concourse.bacc as bacc
    from concourse import mybir as _mybir
    from concourse.bass_utils import run_bass_kernel_spmd

    A = np.asarray
    c = np.ascontiguousarray
    S, B, D = A(x).shape
    E, _, FF = A(L0_ffn_w1).shape
    ipw = A(L0_attn_in_proj_w)
    arrays = {
        "x": c(A(x)),
        "ctxT": c(A(ctx_1024).transpose(2, 0, 1)),
        "w_cross": c(np.stack([A(L0_xattn_Wq), A(L0_xattn_Wk), A(L0_xattn_Wv), A(L0_xattn_Wp).T], axis=1)),
        "w_self": c(np.concatenate([A(L0_attn_w_tor), ipw.T, A(L0_attn_out_w).T], axis=1).reshape(D, 5, D)),
        "cols": c(A(L0_attn_b_tor).reshape(D, 1)),
        "in_bias": c(A(L0_attn_in_proj_b).reshape(1, 3 * D)),
        "rows": c(np.stack([A(L0_xattn_bp), A(L0_attn_out_b), A(L0_ffn_bias)])),
        "exp_idx": c(A(L0_ffn_expert_indices).reshape(S, B, -1).transpose(1, 0, 2)),
        "exp_wt": c(A(L0_ffn_expert_weights).reshape(S, B, -1).transpose(1, 0, 2)),
        "w1": c(A(L0_ffn_w1).transpose(1, 0, 2)),
        "w2": c(A(L0_ffn_w2).reshape(E, FF // 128, 128, D).transpose(2, 0, 1, 3)),
    }
    nc = bacc.Bacc("TRN2", target_bir_lowering=False, num_devices=1)
    args = [nc.dram_tensor(f"in_{n}", arrays[n].shape, _mybir.dt.from_np(arrays[n].dtype), kind="ExternalInput").ap()
            for n in _ORDER]
    out = nc.dram_tensor("out_0", (S, B, D), _mybir.dt.float32, kind="ExternalOutput").ap()
    perceiver_layer(nc, *args, out)
    r = run_bass_kernel_spmd(nc, [{f"in_{n}": arrays[n] for n in _ORDER}], core_ids=[0])
    return r.results[0]["out_0"]
```
